# Optimizing a Trainium2 kernel written in Bass

```python
import numpy as np
import jax
import jax.numpy as jnp

def _softmax(x, axis=-1):
    return jax.nn.softmax(x, axis=axis)

def _gelu(x):
    return jax.nn.gelu(x, approximate=True)

def _silu(x):
    return jax.nn.silu(x)

def _sigmoid(x):
    return jax.nn.sigmoid(x)

def _layernorm(x, axis=-1, eps=1e-05):
    m = jnp.mean(x, axis=axis, keepdims=True)
    v = jnp.var(x, axis=axis, keepdims=True)
    return (x - m) / jnp.sqrt(v + eps)

def _scatter_add(tgt, idx, src, axis=0):
    return tgt.at[idx].add(src)

def _segment_sum(src, seg, n):
    return jax.ops.segment_sum(src, seg, n)
kernel_name = 'mk_gnn_resnorm_d1_gnn_r8_63f9d4'

def setup_inputs(seed: int=0):
    np.random.seed(seed)
    _w = jnp.asarray

    def _rec_inputs():
        import jax
        import jax.numpy as jnp
        _gk = jax.random.key(seed)
        x = -0.000202 + 1 * jax.random.normal(jax.random.fold_in(_gk, 1), (6250, 128), jnp.float32)
        src = jax.random.randint(jax.random.fold_in(_gk, 2), (100000,), 0, 6250, jnp.int32)
        dst = jax.random.randint(jax.random.fold_in(_gk, 3), (100000,), 0, 6250, jnp.int32)
        _o = jnp.argsort(dst, stable=True)
        src = src[_o]
        dst = dst[_o]
        edge_attr_128 = -8.16379e-05 + 0.999858 * jax.random.normal(jax.random.fold_in(_gk, 12), (100000, 128), jnp.float32)
        return (x, src, dst, edge_attr_128)
    x, src, dst, edge_attr_128 = _rec_inputs()

    def _L0_gnn_setup():
        import jax, jax.numpy as jnp
        import numpy as np
        N_NODES = 6250
        N_EDGES = 100000
        D_IN = 128
        N_HEADS = 8
        D_OUT = 16
        key = jax.random.key(seed)
        ks = jax.random.split(key, 10)
        HD = N_HEADS * D_OUT
        nfeat = jax.random.normal(ks[0], (N_NODES, D_IN), dtype=jnp.float32)
        efeat = jax.random.normal(ks[1], (N_EDGES, D_IN), dtype=jnp.float32)
        src = jax.random.randint(ks[2], (N_EDGES,), 0, N_NODES, dtype=jnp.int32)
        dst = jax.random.randint(ks[3], (N_EDGES,), 0, N_NODES, dtype=jnp.int32)
        W_fc = jax.random.normal(ks[4], (D_IN, HD), dtype=jnp.float32) * 0.05
        attn_l = jax.random.normal(ks[5], (N_HEADS, D_OUT), dtype=jnp.float32) * 0.05
        attn_r = jax.random.normal(ks[6], (N_HEADS, D_OUT), dtype=jnp.float32) * 0.05
        bias = jnp.zeros((HD,), dtype=jnp.float32)
        W_e = jax.random.normal(ks[7], (D_IN, HD), dtype=jnp.float32) * 0.05
        b_e = jnp.zeros((HD,), dtype=jnp.float32)
        return {'nfeat': nfeat, 'efeat': efeat, 'src': src, 'dst': dst, 'W_fc': W_fc, 'attn_l': attn_l, 'attn_r': attn_r, 'bias': bias, 'W_e': W_e, 'b_e': b_e}
    _L0_gnn_all = _L0_gnn_setup()
    _L0_gnn_in = {k: v for k, v in _L0_gnn_all.items() if k in ('W_fc', 'attn_l', 'attn_r', 'bias', 'W_e', 'b_e')}
    del _L0_gnn_all
    return {'x': x, 'src': src, 'dst': dst, 'edge_attr_128': edge_attr_128, 'L0_gnn_W_fc': _L0_gnn_in['W_fc'], 'L0_gnn_attn_l': _L0_gnn_in['attn_l'], 'L0_gnn_attn_r': _L0_gnn_in['attn_r'], 'L0_gnn_bias': _L0_gnn_in['bias'], 'L0_gnn_W_e': _L0_gnn_in['W_e'], 'L0_gnn_b_e': _L0_gnn_in['b_e']}

def reference(x, src, dst, edge_attr_128, L0_gnn_W_fc, L0_gnn_attn_l, L0_gnn_attn_r, L0_gnn_bias, L0_gnn_W_e, L0_gnn_b_e):
    import jax
    import jax.numpy as jnp

    def _L0_gnn_ref(nfeat, efeat, src, dst, W_fc, attn_l, attn_r, bias, W_e, b_e):
        import jax, jax.numpy as jnp
        import numpy as np
        N_NODES = 6250
        N_EDGES = 100000
        D_IN = 128
        N_HEADS = 8
        D_OUT = 16
        N = nfeat.shape[0]
        E = src.shape[0]
        H, D = attn_l.shape
        hf = nfeat @ W_fc
        h = hf.reshape(N, H, D)
        el = jnp.einsum('nhd,hd->nh', h, attn_l)
        er = jnp.einsum('nhd,hd->nh', h, attn_r)
        e = jax.nn.leaky_relu(el[src] + er[dst], negative_slope=0.2)
        m = jax.ops.segment_max(e, dst, num_segments=N)
        m = jnp.where(jnp.isfinite(m), m, jnp.zeros_like(m))
        ex = jnp.exp(e - m[dst])
        denom = jax.ops.segment_sum(ex, dst, num_segments=N)
        a = ex / denom[dst]
        agg = jax.ops.segment_sum(a[:, :, None] * h[src], dst, num_segments=N)
        gat = agg.reshape(N, H * D) + bias
        ones = jnp.ones((E,), dtype=nfeat.dtype)
        indeg = jax.ops.segment_sum(ones, dst, num_segments=N)
        sfeat = hf / (indeg + 1.0)[:, None]
        out = gat + sfeat
        ef = efeat @ W_e + b_e
        esum = jax.ops.segment_sum(ef, dst, num_segments=N)
        h_e = esum / jnp.maximum(indeg, 1.0)[:, None]
        return out + h_e
    x = _layernorm(x + _L0_gnn_ref(x, edge_attr_128, src, dst, L0_gnn_W_fc, L0_gnn_attn_l, L0_gnn_attn_r, L0_gnn_bias, L0_gnn_W_e, L0_gnn_b_e), axis=-1)
    return x

_drawn_inputs = setup_inputs


def setup_inputs(seed=0):
    import zlib

    import numpy as np

    out = dict(_drawn_inputs(seed))
    spreads = {'L0_gnn_bias': (0.0, 0.1), 'L0_gnn_b_e': (0.0, 0.1)}
    factors = {'L0_gnn_attn_l': 3.013, 'L0_gnn_attn_r': 8.0}
    for name, (base, spread) in spreads.items():
        noise = np.random.default_rng([zlib.crc32(name.encode()), seed]).standard_normal(out[name].shape)
        drawn = base * np.exp(spread * noise) if base else spread * noise
        out[name] = jnp.asarray(drawn.astype(out[name].dtype))
    for name, factor in factors.items():
        out[name] = (out[name] * factor).astype(out[name].dtype)
    return out
```

```python
import numpy as np
import concourse.bass as bass
from concourse import mybir
from contextlib import ExitStack

F32 = mybir.dt.float32
I32 = mybir.dt.int32
ALU = mybir.AluOpType
ACT = mybir.ActivationFunctionType
AX = mybir.AxisListType

P = 128
BIG = float(2.0 ** 100)
DEN_FLOOR = 1e-30
LN_EPS = 1e-5
SLOPE = 0.2


class Chain:

    def __init__(self, eng, sem, base):
        self.eng, self.sem, self.base, self.n = eng, sem, base, 0

    def done(self, ins):
        ins.then_inc(self.sem, 1)
        self.n += 1

    def after(self):
        self.eng.wait_ge(self.sem, self.base + self.n)


def gat_layer(nc, x, src, dst, ef, w_fc, attn_l, attn_r, bias, w_e, b_e, out):
    N, D = x.shape
    H, DH = attn_l.shape
    EPAD = src.shape[0]
    ET = EPAD // P
    NT = -(-N // P)
    TAIL = N - (NT - 1) * P
    MC = 16
    COLS = ET + NT + (-(ET + NT)) % MC
    NM = COLS // MC
    NB = -(-COLS // P)
    CP = NB * P
    KD = NT
    RING = 3
    Q = 4
    QC = MC // Q
    ONE, HF, EX, ROW = D, D + 1, 2 * D + 1, 2 * D + 1 + H
    RS = ROW + 1
    TW = D + H
    WC = D + 2 * H
    assert NM == 1 + RING * ((NM - 1) // RING) and MC * H == P
    XC = 4
    NXC = (NT - 1) // XC
    assert NXC % 2 == 0 and NXC * XC == NT - 1
    EB = 7
    NEB = NT // EB
    assert NEB * EB == NT

    with ExitStack() as ctx:
        def sb(name, shape, dt=F32):
            return ctx.enter_context(nc.sbuf_tensor(name, shape, dt))

        def sem(name):
            return ctx.enter_context(nc.semaphore(name))

        ctx.enter_context(nc.allow_non_contiguous_dma(reason="small tables, and one column of dst"))
        node_table = nc.dram_tensor("node_table", (N, TW), F32, kind="Internal").ap()
        tk_dram = nc.dram_tensor("tk_dram", (2, CP), I32, kind="Internal").ap()

        acc = sb("acc", [P, (NT + 1) * RS])
        rows = sb("rows", [P, RING, MC, RS])
        S = sb("S", [P, RING, MC, P])
        ST = sb("ST", [P, MC, P])
        er_tab = sb("er_tab", [P, (NT + 1) * H])
        ident = sb("ident", [P, P])
        iota_row = sb("iota_row", [P, P])
        ones_row = sb("ones_row", [1, P])
        dlocT = sb("dlocT", [P, CP])
        lastT = sb("lastT", [P, CP])
        startT = sb("startT", [P, CP])
        srcT = sb("srcT", [P, CP], I32)
        kmask = sb("kmask", [P, 3, CP])
        ktab = sb("ktab", [1, CP], I32)
        ttab = sb("ttab", [1, CP], I32)
        src_now = sb("src_now", [P, RING, MC], I32)
        start_rep = sb("start_rep", [P, MC, H])
        el_now = sb("el_now", [P, MC, H])
        startS = sb("startS", [P, P])
        runmax = sb("runmax", [P, P])
        V = sb("V", [P, MC, H + 1])
        absent = sb("absent", [P, MC])
        muH = sb("muH", [P, H, MC])
        kf_rep = sb("kf_rep", [P, H, MC])
        kb_rep = sb("kb_rep", [P, H, MC])
        upmax = sb("upmax", [P, P])
        MH = sb("MH", [P, H, MC])
        carry = sb("carry", [P, H])
        m_old = sb("m_old", [P, H])
        fz = sb("fz", [P, 2, H])
        fl = sb("fl", [P, 2, H])
        fd = sb("fd", [P, H])
        fac = sb("fac", [P, H])
        erS = sb("erS", [P, P])
        zz = sb("zz", [P, 2, P])
        zl = sb("zl", [P, 2, P])
        zd = sb("zd", [P, P])
        w_sb = sb("w_sb", [P, WC])
        we_sb = sb("we_sb", [P, D])
        attn_b = sb("attn_b", [P, 2, D])
        wa = sb("wa", [P, 2, D])
        bias_b = sb("bias_b", [P, D])
        be_b = sb("be_b", [P, D])
        xin = S[:, 0, 0:2 * XC, :].rearrange("p (h c) d -> p h c d", h=2)
        xT = S[:, 1, 0:2 * XC, :].rearrange("p (h c) d -> p h c d", h=2)
        stage = S[:, 2, :, :].rearrange("p a b -> p (a b)")[:, 0:2 * XC * TW].rearrange("p (h c d) -> p h c d", h=2, c=XC)
        flat = rows[:, :, :, :].rearrange("p a b c -> p (a b c)")
        W7 = NB * P

        def piece(n, width=W7):
            return flat[:, n * W7:n * W7 + width]

        dcol_i = piece(0).bitcast(I32).rearrange("p (b e) -> p b e", e=P)
        scol_i = piece(1).bitcast(I32).rearrange("p (b e) -> p b e", e=P)
        dcol = piece(2).rearrange("p (b e) -> p b e", e=P)
        scol = piece(3).rearrange("p (b e) -> p b e", e=P)
        dloc = piece(4).rearrange("p (b e) -> p b e", e=P)
        lastc = piece(5).rearrange("p (b e) -> p b e", e=P)
        startc = piece(6).rearrange("p (b e) -> p b e", e=P)
        stb = piece(7)
        cmp_t = piece(8)
        first_i = piece(9)[0:1, :].bitcast(I32)
        tile_i = piece(10)[0:1, :].bitcast(I32)
        first_s = piece(11)[0:1, :]
        krow = flat[0:1, 12 * W7:12 * W7 + CP]
        kmrow = acc[0:1, 0:3 * CP].rearrange("p (a c) -> p a c", a=3)
        sid_i = sb("sid_i", [P, NB], I32)
        sid = sb("sid", [P, NB])
        tcnt = sb("tcnt", [P, NB])
        kcol = sb("kcol", [P, NB])
        k128 = sb("k128", [P, NB])
        t_i = sb("t_i", [P, NB], I32)
        k_i = sb("k_i", [P, NB], I32)

        def bank(name):
            return ctx.enter_context(nc.psum_tensor(name, [P, 512], F32))

        ps_main = [bank("ps_main0"), bank("ps_main1")]
        ps_st = [bank("ps_st0"), bank("ps_st1")]
        ps_x = bank("ps_x")
        ps_f = bank("ps_f")
        ps_e = bank("ps_e")
        ps_t = bank("ps_t")
        el_t, start_t = ps_x[:, 0:P], ps_x[:, P:2 * P]
        run_e, mu = ps_f[:, 0:P], ps_f[:, P:P + MC * (H + 1)]
        er_e, mx_e = ps_e[:, 0:P], ps_e[:, P:2 * P]

        s_id0, s_id, s_iota, s_one = sem("s_id0"), sem("s_id"), sem("s_iota"), sem("s_one")
        s_w, s_bias, s_first = sem("s_w"), sem("s_bias"), sem("s_first")
        s_wcat = sem("s_wcat")
        s_xz = sem("s_xz")
        s_x = [sem("s_x0"), sem("s_x1")]
        s_xt, s_xtc, s_hf, s_hfc = sem("s_xt"), sem("s_xtc"), sem("s_hf"), sem("s_hfc")
        s_er = sem("s_er")
        s_tab = [sem("s_tab0"), sem("s_tab1")]
        s_pre = sem("s_pre")
        s_stb, s_stbc = sem("s_stb"), sem("s_stbc")
        s_ti, s_dg, s_sg, s_tk, s_tkr = sem("s_ti"), sem("s_dg"), sem("s_sg"), sem("s_tk"), sem("s_tkr")
        s_cols = sem("s_cols")
        s_tt, s_ttc = sem("s_tt"), sem("s_ttc")
        s_kmr, s_km, s_kmc = sem("s_kmr"), sem("s_km"), sem("s_kmc")
        s_init = sem("s_init")
        s_idx, s_tick = sem("s_idx"), sem("s_tick")
        s_g = [sem(f"s_g{r}") for r in range(RING)]
        s_ef = [sem(f"s_ef{r}") for r in range(RING)]
        s_prep, s_S = sem("s_prep"), sem("s_S")
        s_stp, s_st = sem("s_stp"), sem("s_st")
        s_ere, s_ers = sem("s_ere"), sem("s_ers")
        s_elc = sem("s_elc")
        s_elt, s_starts, s_run, s_rune = sem("s_elt"), sem("s_starts"), sem("s_run"), sem("s_rune")
        s_V, s_mu, s_MH, s_mxe = sem("s_V"), sem("s_mu"), sem("s_MH"), sem("s_mxe")
        s_fd, s_fac, s_zd, s_ex, s_prod = sem("s_fd"), sem("s_fac"), sem("s_zd"), sem("s_ex"), sem("s_prod")
        s_soft = sem("s_soft")
        s_mm, s_fl = sem("s_mm"), sem("s_fl")
        s_lx, s_ep = sem("s_lx"), sem("s_ep")
        s_es, s_est, s_estc, s_he, s_o, s_out = sem("s_es"), sem("s_est"), sem("s_estc"), sem("s_he"), sem("s_o"), sem("s_out")
        s_sq, s_var, s_std, s_rt = sem("s_sq"), sem("s_var"), sem("s_std"), sem("s_rt")
        block = ctx.enter_context(nc.Block())

        def fin(n):
            return flat[:, n * EB * D:(n + 1) * EB * D].rearrange("p (k d) -> p k d", d=D)

        x_f, hf_f, es_f, o_f, t_f = fin(0), fin(1), fin(2), fin(3), fin(4)
        esT_f = fin(5)
        sm = flat[:, 6 * EB * D:6 * EB * D + 128]

        def small(n):
            return sm[:, n * EB:(n + 1) * EB]

        den_f = flat[:, 6 * EB * D + 128:6 * EB * D + 128 + EB * H].rearrange("p (k h) -> p k h", h=H)
        rden_f = flat[:, 6 * EB * D + 256:6 * EB * D + 256 + EB * H].rearrange("p (k h) -> p k h", h=H)

        G16 = MC * 16

        @block.sync
        def _(sp):
            sp.dma_start(w_sb[:, 0:D], w_fc[:, :]).then_inc(s_w, 16)
            sp.dma_start(attn_b[:, 0, :], attn_l.rearrange("h d -> (h d)").partition_broadcast(P)).then_inc(s_w, 16)
            sp.dma_start(attn_b[:, 1, :], attn_r.rearrange("h d -> (h d)").partition_broadcast(P)).then_inc(s_w, 16)
            sp.dma_start(first_i[:, 0:ET], dst.rearrange("(a t e) -> a t e", a=1, e=P)[:, :, 0]).then_inc(s_first, 16)
            def load_x(c, h):
                sp.dma_start(xin[:, h, :, :],
                             x[bass.ds(c * (XC * P), XC * P), :].rearrange("(k p) d -> p k d", p=P)).then_inc(s_x[h], 16)

            def store_table(c, h):
                sp.wait_ge(s_er, (c + 1) * 2)
                sp.dma_start(node_table[bass.ds(c * (XC * P), XC * P), :].rearrange("(k p) w -> p k w", p=P),
                             stage[:, h, :, :]).then_inc(s_tab[h], 16)

            load_x(0, 0)
            load_x(1, 1)
            with sp.Fori(0, NXC // 2 - 1) as i:
                for h in range(2):
                    store_table(i * 2 + h, h)
                    load_x(i * 2 + (h + 2), h)
            for h in range(2):
                store_table(NXC - 2 + h, h)
            sp.wait_ge(s_xz, 1)
            sp.dma_start(xin[0:TAIL, 0, 0, :], x[NXC * XC * P:N, :]).then_inc(s_x[0], 16)
            sp.wait_ge(s_er, NXC * 2 + 1)
            sp.dma_start(node_table[NXC * XC * P:N, :], stage[0:TAIL, 0, 0, :]).then_inc(s_tab[0], 16)
            sp.dma_start(we_sb[:, :], w_e[:, :]).then_inc(s_bias, 16)
            sp.dma_start(bias_b[:, :], bias.partition_broadcast(P)).then_inc(s_bias, 16)
            sp.dma_start(be_b[:, :], b_e.partition_broadcast(P)).then_inc(s_bias, 16)
            sp.wait_ge(s_ti, 1)
            sp.dma_start(tk_dram[0, :].rearrange("(b p) -> p b", p=P), t_i[:, :]).then_inc(s_tk, 16)
            sp.dma_start(tk_dram[1, :].rearrange("(b p) -> p b", p=P), k_i[:, :]).then_inc(s_tk, 16)
            sp.wait_ge(s_tk, 32)
            sp.dma_start(ttab[:, :], tk_dram[0:1, :]).then_inc(s_tkr, 16)
            sp.dma_start(ktab[:, :], tk_dram[1:2, :]).then_inc(s_tkr, 16)
            sp.wait_ge(s_tkr, 32)
            sp.wait_ge(s_init, 1)

            def load_ef(m, r, first):
                for q in range(Q):
                    cols = range(q * QC, (q + 1) * QC)
                    ts = [sp.value_load(ttab[0:1, bass.ds(m * MC + c, 1)], min_val=0, max_val=ET - 1) for c in cols]
                    if not first:
                        sp.wait_ge(s_mm, (m - RING) * MC + (q + 1) * QC)
                    for c, t in zip(cols, ts):
                        sp.dma_start(rows[:, r, c, 0:D], ef[bass.ds(t * P, P), :]).then_inc(s_ef[r], 16)

            for m in range(RING + 1):
                load_ef(m, m % RING, m < RING)
            with sp.Fori(0, (NM - 1 - RING) // RING) as i:
                for j in range(RING):
                    load_ef(i * RING + (RING + 1 + j), (1 + j) % RING, False)
            def load_fin(b, whole):
                for buf, table in ((x_f, x), (hf_f, node_table)):
                    if whole:
                        sp.dma_start(buf[:, :, :], table[bass.ds(b * (EB * P), EB * P), 0:D]
                                     .rearrange("(k p) d -> p k d", p=P)).then_inc(s_lx, 16)
                    else:
                        sp.dma_start(buf[:, 0:EB - 1, :], table[b * EB * P:(NT - 1) * P, 0:D]
                                     .rearrange("(k p) d -> p k d", p=P)).then_inc(s_lx, 16)
                        sp.dma_start(buf[0:TAIL, EB - 1, :], table[(NT - 1) * P:N, 0:D]).then_inc(s_lx, 16)

            sp.wait_ge(s_fl, COLS + 2)
            load_fin(0, True)

            def store_fin(b):
                sp.wait_ge(s_o, b + 1)
                sp.dma_start(out[bass.ds(b * (EB * P), EB * P), :].rearrange("(k p) d -> p k d", p=P),
                             o_f[:, :, :]).then_inc(s_out, 16)

            with sp.Fori(0, NEB - 2) as b:
                store_fin(b)
                load_fin(b + 1, True)
            store_fin(NEB - 2)
            load_fin(NEB - 1, False)
            sp.wait_ge(s_o, NEB)
            sp.dma_start(out[(NEB - 1) * EB * P:(NT - 1) * P, :].rearrange("(k p) d -> p k d", p=P),
                         o_f[:, 0:EB - 1, :]).then_inc(s_out, 16)
            sp.dma_start(out[(NT - 1) * P:N, :], o_f[0:TAIL, EB - 1, :]).then_inc(s_out, 16)
            sp.wait_ge(s_out, (NEB + 1) * 16)

        @block.gpsimd
        def _(pool):
            nc.gpsimd.memset(ident[:, :], 0.0).then_inc(s_id0, 1)
            pool.wait_ge(s_id0, 1)
            nc.gpsimd.affine_select(out=ident[:, :], in_=ident[:, :], compare_op=ALU.not_equal, fill=1.0, base=0,
                                    pattern=[[-1, P]], channel_multiplier=1).then_inc(s_id, 1)
            nc.gpsimd.iota(iota_row[:, :], [[1, P]], base=0, channel_multiplier=0,
                           allow_small_or_imprecise_dtypes=True).then_inc(s_iota, 1)
            nc.gpsimd.iota(tile_i[:, :], [[1, CP]], base=0, channel_multiplier=0).then_inc(s_iota, 1)
            nc.gpsimd.iota(sid_i[:, :], [[P, NB]], base=0, channel_multiplier=1).then_inc(s_iota, 1)
            pool.wait_ge(s_ti, 1)
            for b in range(NB):
                for table, into, s in ((dst, dcol_i, s_dg), (src, scol_i, s_sg)):
                    nc.gpsimd.indirect_dma_start(
                        out=into[:, b, :], out_offset=None, in_=table.rearrange("(t e) -> t e", e=P),
                        in_offset=bass.IndirectOffsetOnAxis(ap=t_i[:, b:b + 1], axis=0)).then_inc(s, 16)
            pool.wait_ge(s_ttc, 4 * NB)
            pool.wait_ge(s_init, 1)
            pool.wait_ge(s_tab[0], (NXC // 2 + 1) * 16)
            pool.wait_ge(s_tab[1], (NXC // 2) * 16)

            def gather(m, r, first):
                for q in range(Q):
                    if not first:
                        pool.wait_ge(s_mm, (m - RING) * MC + (q + 1) * QC)
                        pool.sem_inc(s_tick, 1)
                    if q == 0:
                        nc.gpsimd.tensor_copy(src_now[:, r, :], srcT[:, bass.ds(m * MC, MC)]).then_inc(s_idx, 1)
                        pool.wait_ge(s_idx, m + 1)
                        pool.sem_inc(s_tick, 1)
                    for c in range(q * QC, (q + 1) * QC):
                        nc.gpsimd.indirect_dma_start(
                            out=rows[:, r, c, HF:ROW], out_offset=None, in_=node_table[:, :],
                            in_offset=bass.IndirectOffsetOnAxis(ap=src_now[:, r, c:c + 1], axis=0)).then_inc(s_g[r], 16)

            for m in range(RING + 1):
                gather(m, m % RING, m < RING)
            with pool.Fori(0, (NM - 1 - RING) // RING) as i:
                for j in range(RING):
                    gather(i * RING + (RING + 1 + j), (1 + j) % RING, False)

        @block.tensor
        def _(pe):
            pe.wait_ge(s_id, 1)
            pe.wait_ge(s_one, 1)
            pe.wait_ge(s_wcat, 1)

            def project(c, h, tiles):
                for a in range(tiles):
                    last = nc.tensor.transpose(ps_st[h][:, a * P:(a + 1) * P], xin[:, h, a, :], ident[:, :])
                    last.then_inc(s_xt, 1)
                pe.wait_ge(s_xtc, c + 1)
                for a in range(tiles):
                    if a % 2 == 0:
                        pe.wait_ge(s_hfc, c * 2 + a // 2 + 1)
                    o = ps_main[a // 2][:, (a % 2) * WC:(a % 2) * WC + WC]
                    nc.tensor.matmul(o, xT[:, h, a, :], w_sb[:, 0:WC], start=True, stop=True).then_inc(s_hf, 1)

            with pe.Fori(0, NXC // 2) as i:
                for h in range(2):
                    pe.wait_ge(s_x[h], i * 16 + 16)
                    project(i * 2 + h, h, XC)
            pe.wait_ge(s_x[0], (NXC // 2 + 1) * 16)
            project(NXC, 0, 1)
            pe.wait_ge(s_stb, 1)
            nc.tensor.matmul(ps_x[:, 0:ET // 2], ones_row[:, :], first_s[:, 0:ET // 2], start=True, stop=True)
            nc.tensor.matmul(ps_f[:, 0:ET // 2], ones_row[:, :], first_s[:, ET // 2:2 * (ET // 2)],
                             start=True, stop=True).then_inc(s_stbc, 1)
            pe.wait_ge(s_cols, 1)
            n = 0
            for b in range(NB):
                for table in (dloc, lastc, startc, scol):
                    if n >= 1:
                        pe.wait_ge(s_ttc, n)
                    nc.tensor.transpose(ps_t[:, 0:P], table[:, b, :], ident[:, :]).then_inc(s_tt, 1)
                    n += 1
            pe.wait_ge(s_kmr, 1)
            half = CP // 2
            for a in range(3):
                for j in range(2):
                    n = a * 2 + j
                    if n >= 2:
                        pe.wait_ge(s_kmc, n - 1)
                    nc.tensor.matmul(ps_main[n % 2][:, 0:half], ones_row[:, :], kmrow[:, a, j * half:(j + 1) * half],
                                     start=True, stop=True).then_inc(s_km, 1)
            pe.wait_ge(s_init, 1)

            def prepare(m, r):
                ks = [pe.value_load(ktab[0:1, bass.ds(m * MC + c, 1)], min_val=0, max_val=KD) for c in range(MC)]
                pe.wait_ge(s_S, m + 1)
                for q in range(Q):
                    pe.wait_ge(s_st, m * Q + q + 1)
                    for a in range(QC):
                        last = nc.tensor.transpose(ps_st[q % 2][:, a * P:(a + 1) * P], S[:, r, q * QC + a, :], ident[:, :])
                    last.then_inc(s_stp, 1)
                pe.wait_ge(s_st, m * Q + Q + 2)
                pe.wait_ge(s_ers, m + 1)
                for c in range(MC):
                    last = nc.tensor.matmul(er_e[:, c * H:(c + 1) * H], ST[:, c, :], er_tab[:, bass.ds(ks[c] * H, H)],
                                            start=True, stop=True)
                last.then_inc(s_ere, 1)

            def slot(u, r, rm, round_m, chain, main):
                if chain:
                    pe.wait_ge(s_prep, u * 3 + 3)
                    nc.tensor.transpose(start_t, start_rep[:, :, :].rearrange("p c h -> p (c h)"), ident[:, :])
                    pe.wait_ge(s_elc, u + 1)
                    nc.tensor.transpose(el_t, el_now[:, :, :].rearrange("p c h -> p (c h)"), ident[:, :]).then_inc(s_elt, 1)
                if main:
                    main_q(u - 1, rm, round_m, 0)
                if chain:
                    pe.wait_ge(s_run, u + 1)
                    nc.tensor.transpose(run_e, runmax[:, :], ident[:, :]).then_inc(s_rune, 1)
                if main:
                    main_q(u - 1, rm, round_m, 1)
                if chain:
                    pe.wait_ge(s_V, u * 2 + 2)
                    for c in range(MC):
                        last = nc.tensor.matmul(mu[:, c * (H + 1):(c + 1) * (H + 1)], S[:, r, c, :], V[:, c, :],
                                                start=True, stop=True)
                    last.then_inc(s_mu, 1)
                if main:
                    main_q(u - 1, rm, round_m, 2)
                if chain:
                    pe.wait_ge(s_MH, u + 1)
                    for c in range(MC):
                        last = nc.tensor.matmul(mx_e[:, c * H:(c + 1) * H], ST[:, c, :], MH[:, :, c],
                                                start=True, stop=True)
                    last.then_inc(s_mxe, 1)
                if main:
                    main_q(u - 1, rm, round_m, 3)
                if chain:
                    prepare(u + 1, (r + 1) % RING)

            def main_q(m, r, round_m, q):
                if q == 0:
                    pe.wait_ge(s_ef[r], round_m)
                pe.wait_ge(s_prod, m * Q + q + 1)
                for c in range(q * QC, (q + 1) * QC):
                    pe.wait_ge(s_fl, m * MC + c + 1)
                    last = nc.tensor.matmul(ps_main[c % 2][:, 0:ROW], S[:, r, c, :], rows[:, r, c, 0:ROW],
                                            start=True, stop=True)
                    last.then_inc(s_mm, 1)

            prepare(0, 0)
            slot(0, 0, None, None, True, False)
            with pe.Fori(0, (NM - 1) // RING) as i:
                for j in range(RING):
                    slot(i * RING + (1 + j), (1 + j) % RING, j, i * G16 + G16, True, True)
            slot(NM, None, (NM - 1) % RING, ((NM - 1) // RING + 1) * G16, False, True)

            pe.wait_ge(s_bias, 48)

            def edge_part(b):
                pe.wait_ge(s_es, b + 1)
                for a in range(EB):
                    nc.tensor.transpose(ps_st[a // 4][:, (a % 4) * P:(a % 4 + 1) * P], es_f[:, a, :],
                                        ident[:, :]).then_inc(s_est, 1)
                pe.wait_ge(s_estc, 2 * b + 2)
                for a in range(EB):
                    nc.tensor.matmul(ps_main[a // 4][:, (a % 4) * P:(a % 4 + 1) * P], esT_f[:, a, :], we_sb[:, :],
                                     start=True, stop=True).then_inc(s_he, 1)

            with pe.Fori(0, NEB) as b:
                edge_part(b)

        @block.scalar
        def _(act):
            def table_rows(c, h, tiles):
                act.wait_ge(s_xt, c * XC + tiles)
                nc.scalar.activation(xT[:, h, 0:tiles, :].rearrange("p k d -> p (k d)"),
                                     ps_st[h][:, 0:tiles * P], ACT.Copy).then_inc(s_xtc, 1)

            with act.Fori(0, NXC // 2) as i:
                for h in range(2):
                    table_rows(i * 2 + h, h, XC)
            table_rows(NXC, 0, 1)
            n = 0
            for b in range(NB):
                for table in (dlocT, lastT, startT, srcT):
                    act.wait_ge(s_tt, n + 1)
                    nc.scalar.activation(table[:, b * P:(b + 1) * P], ps_t[:, 0:P], ACT.Copy).then_inc(s_ttc, 1)
                    n += 1
            half = CP // 2
            for a in range(3):
                for j in range(2):
                    n = a * 2 + j
                    act.wait_ge(s_km, n + 1)
                    nc.scalar.activation(kmask[:, a, j * half:(j + 1) * half], ps_main[n % 2][:, 0:half],
                                         ACT.Copy).then_inc(s_kmc, 1)

            act.sem_inc(s_st, 2)
            act.sem_inc(s_ers, 1)

            def prepare(m):
                act.wait_ge(s_mxe, m + 1)
                for q in range(Q):
                    act.wait_ge(s_stp, m * Q + q + 1)
                    nc.scalar.activation(ST[:, q * QC:(q + 1) * QC, :].rearrange("p c n -> p (c n)"),
                                         ps_st[q % 2][:, :], ACT.Copy).then_inc(s_st, 1)
                act.wait_ge(s_ere, m + 1)
                act.wait_ge(s_zd, m + 1)
                nc.scalar.activation(erS[:, :], er_e, ACT.Copy).then_inc(s_ers, 1)

            def softmax(m, r, round_g):
                act.wait_ge(s_g[r], round_g)
                nc.scalar.activation(el_now[:, :, :], rows[:, r, :, EX:ROW], ACT.Copy).then_inc(s_elc, 1)
                act.wait_ge(s_elt, m + 1)
                nc.scalar.activation(startS[:, :], start_t, ACT.Copy).then_inc(s_starts, 1)
                act.wait_ge(s_fd, m + 1)
                nc.scalar.activation(fac[:, :], fd[:, :], ACT.Exp).then_inc(s_fac, 1)
                act.wait_ge(s_zd, m + 2)
                nc.scalar.activation(rows[:, r, :, EX:ROW], zd[:, :].rearrange("p (c h) -> p c h", h=H),
                                     ACT.Exp).then_inc(s_ex, 1)

            act.sem_inc(s_mxe, 1)
            prepare(0)
            softmax(0, 0, G16)
            prepare(1)
            with act.Fori(0, (NM - 1) // RING) as i:
                for j in range(RING):
                    softmax(i * RING + (1 + j), (1 + j) % RING, i * G16 + (1 + (1 + j) // RING) * G16)
                    prepare(i * RING + (2 + j))

            def last_stage(b):
                for a, tiles in ((0, 4), (1, EB - 4)):
                    act.wait_ge(s_est, b * EB + (4 if a == 0 else EB))
                    nc.scalar.activation(esT_f[:, 4 * a:4 * a + tiles, :].rearrange("p k d -> p (k d)"),
                                         ps_st[a][:, 0:tiles * P], ACT.Copy).then_inc(s_estc, 1)
                act.wait_ge(s_sq, b + 1)
                nc.scalar.activation(t_f[:, :, :], o_f[:, :, :], ACT.Square).then_inc(s_var, 1)
                act.wait_ge(s_std, b + 1)
                nc.scalar.activation(small(7), small(6), ACT.Sqrt).then_inc(s_rt, 1)

            with act.Fori(0, NEB) as b:
                last_stage(b)

        @block.vector
        def _(dve):
            pre = Chain(dve, s_pre, 0)
            nc.vector.memset(ones_row[:, :], 1.0).then_inc(s_one, 1)
            dve.wait_ge(s_w, 48)
            for a in range(2):
                pre.done(nc.vector.tensor_tensor(wa[:, a, :], w_sb[:, 0:D], attn_b[:, a, :], ALU.mult))
            pre.after()
            nc.vector.tensor_reduce(w_sb[:, D:WC].rearrange("p (a h) -> p a h", h=H),
                                    wa[:, :, :].rearrange("p a (h d) -> p a h d", d=DH),
                                    AX.X, ALU.add).then_inc(s_wcat, 1)
            dve.wait_ge(s_first, 16)
            dve.wait_ge(s_iota, 3)
            pre.done(nc.vector.tensor_single_scalar(first_i[:, 0:ET], first_i[:, 0:ET], P.bit_length() - 1,
                                                    ALU.arith_shift_right))
            pre.after()
            nc.vector.tensor_tensor(first_s[:, 0:ET], first_i[:, 0:ET], tile_i[:, 0:ET], ALU.add).then_inc(s_stb, 1)
            pre.done(nc.vector.tensor_copy(sid[:, :], sid_i[:, :]))

            pre.done(nc.vector.memset(er_tab[:, NT * H:(NT + 1) * H], 0.0))
            dve.sem_inc(s_hfc, 2)

            def results(c, h, tiles):
                for g in range(-(-tiles // 2)):
                    k = min(2, tiles - 2 * g)
                    dve.wait_ge(s_hf, c * XC + 2 * g + k)
                    v = ps_main[g][:, 0:k * WC].rearrange("p (k w) -> p k w", w=WC)
                    nc.vector.tensor_copy(stage[:, h, 2 * g:2 * g + k, :], v[:, :, 0:TW]).then_inc(s_er, 1)
                    nc.vector.tensor_scalar(er_tab[:, bass.ds((c * XC + 2 * g) * H, k * H)]
                                            .rearrange("p (k h) -> p k h", h=H), v[:, :, TW:WC], 1.0, None,
                                            ALU.mult).then_inc(s_hfc, 1)

            for h in range(2):
                results(h, h, XC)
            with dve.Fori(1, NXC // 2) as i:
                for h in range(2):
                    dve.wait_ge(s_tab[h], i * 16)
                    results(i * 2 + h, h, XC)
            dve.wait_ge(s_xt, NXC * XC)
            nc.vector.memset(xin[:, 0, 0, :], 0.0).then_inc(s_xz, 1)
            dve.wait_ge(s_tab[0], NXC // 2 * 16)
            results(NXC, 0, 1)

            dve.wait_ge(s_stbc, 1)
            for j, p_ in enumerate((ps_x, ps_f)):
                pre.done(nc.vector.tensor_copy(stb[:, j * (ET // 2):(j + 1) * (ET // 2)], p_[:, 0:ET // 2]))
            for b in range(NB):
                pre.after()
                pre.done(nc.vector.tensor_scalar(cmp_t[:, 1:ET], stb[:, 1:ET], sid[:, b:b + 1], None, ALU.is_le))
                pre.after()
                pre.done(nc.vector.tensor_reduce(tcnt[:, b:b + 1], cmp_t[:, 1:ET], AX.X, ALU.add))
            pre.after()
            pre.done(nc.vector.tensor_tensor(kcol[:, :], sid[:, :], tcnt[:, :], ALU.subtract))
            pre.after()
            pre.done(nc.vector.tensor_scalar(kcol[:, :], kcol[:, :], float(KD), None, ALU.min))
            pre.done(nc.vector.tensor_copy(t_i[:, :], tcnt[:, :]))
            pre.after()
            pre.done(nc.vector.tensor_scalar(k128[:, :], kcol[:, :], float(P), None, ALU.mult))
            pre.done(nc.vector.tensor_copy(k_i[:, :], kcol[:, :]))
            pre.after()
            dve.sem_inc(s_ti, 1)

            dve.wait_ge(s_dg, NB * 16)
            pre.done(nc.vector.tensor_copy(dcol, dcol_i))
            dve.wait_ge(s_sg, NB * 16)
            pre.done(nc.vector.tensor_copy(scol, scol_i))
            pre.after()
            pre.done(nc.vector.tensor_tensor(dloc, dcol, k128[:, :].unsqueeze(2).to_broadcast([P, NB, P]), ALU.subtract))
            pre.done(nc.vector.tensor_tensor(lastc[:, :, 0:P - 1], dcol[:, :, 0:P - 1], dcol[:, :, 1:P], ALU.not_equal))
            pre.done(nc.vector.memset(lastc[:, :, P - 1:P], 1.0))
            pre.after()
            pre.done(nc.vector.tensor_scalar(startc[:, :, 1:P], lastc[:, :, 0:P - 1], -BIG, None, ALU.mult))
            pre.done(nc.vector.memset(startc[:, :, 0:1], -BIG))
            pre.after()
            dve.sem_inc(s_cols, 1)

            dve.wait_ge(s_tkr, 32)
            pre.done(nc.vector.tensor_copy(krow, ktab[:, :]))
            pre.after()
            pre.done(nc.vector.tensor_tensor(kmrow[:, 0, 1:CP], krow[:, 1:CP], krow[:, 0:CP - 1], ALU.not_equal))
            pre.done(nc.vector.memset(kmrow[:, 0, 0:1], 1.0))
            pre.after()
            pre.done(nc.vector.tensor_scalar(kmrow[:, 1, :], kmrow[:, 0, :], -BIG, None, ALU.mult))
            pre.done(nc.vector.tensor_scalar(kmrow[:, 2, 0:CP - 1], kmrow[:, 0, 1:CP], -BIG, None, ALU.mult))
            pre.after()
            pre.done(nc.vector.tensor_copy(kmrow[:, 0, :], kmrow[:, 1, :]))
            pre.after()
            by_macro = kmrow.rearrange("p a (m c) -> p a m c", c=MC)
            pre.done(nc.vector.memset(by_macro[:, 1, :, 0:1], -BIG))
            pre.done(nc.vector.memset(by_macro[:, 2, :, MC - 1:MC], -BIG))
            pre.after()
            dve.sem_inc(s_kmr, 1)

            dve.wait_ge(s_ttc, 4 * NB)
            dve.wait_ge(s_kmc, 6)
            dve.wait_ge(s_tab[0], (NXC // 2 + 1) * 16)
            dve.wait_ge(s_tab[1], NXC // 2 * 16)
            pre.done(nc.vector.memset(acc[:, :], 0.0))
            pre.done(nc.vector.memset(rows[:, :, :, ONE:ONE + 1], 1.0))
            pre.done(nc.vector.memset(carry[:, :], -BIG))
            pre.after()
            dve.sem_inc(s_init, 1)
            dve.sem_inc(s_fl, 2)
            dve.sem_inc(s_zd, 1)

            def build(m, r):
                cols = bass.ds(m * MC, MC)
                for rep_, table in ((kf_rep, kmask[:, 1, cols]), (kb_rep, kmask[:, 2, cols])):
                    nc.vector.tensor_scalar(rep_[:, :, :], table.unsqueeze(1).to_broadcast([P, H, MC]), 1.0, None,
                                            ALU.mult).then_inc(s_prep, 1)
                nc.vector.tensor_scalar(start_rep[:, :, :], startT[:, cols].unsqueeze(2).to_broadcast([P, MC, H]), 1.0,
                                        None, ALU.mult).then_inc(s_prep, 1)
                nc.vector.tensor_tensor(S[:, r, :, :], iota_row[:, :].unsqueeze(1).to_broadcast([P, MC, P]),
                                        dlocT[:, cols].unsqueeze(2).to_broadcast([P, MC, P]),
                                        ALU.is_equal).then_inc(s_S, 1)

            def add_in(m, q):
                cs = range(q * QC, (q + 1) * QC)
                ks = [dve.value_load(ktab[0:1, bass.ds(m * MC + c, 1)], min_val=0, max_val=KD) for c in cs]
                for c, k in zip(cs, ks):
                    dve.wait_ge(s_mm, m * MC + (c + 1))
                    dve.wait_ge(s_fl, m * MC + (c + 2))
                    a = acc[:, bass.ds(k * RS, ROW)]
                    nc.vector.tensor_tensor(a, a, ps_main[c % 2][:, 0:ROW], ALU.add).then_inc(s_fl, 1)

            SOFT = 15

            def slot(u, r, chain, main):
                if chain:
                    cols = bass.ds(u * MC, MC)
                    soft = Chain(dve, s_soft, u * SOFT)
                    dve.wait_ge(s_starts, u + 1)
                    nc.vector.tensor_tensor_scan(runmax[:, :], startS[:, :], el_t, -BIG, ALU.add, ALU.max).then_inc(s_run, 1)
                if main:
                    add_in(u - 1, 0)
                if chain:
                    last = lastT[:, cols].unsqueeze(2)
                    dve.wait_ge(s_rune, u + 1)
                    nc.vector.tensor_tensor(V[:, :, 0:H], run_e.rearrange("p (c h) -> p c h", h=H),
                                            last.to_broadcast([P, MC, H]), ALU.mult).then_inc(s_V, 1)
                    nc.vector.tensor_scalar(V[:, :, H:H + 1], last, 1.0, None, ALU.mult).then_inc(s_V, 1)
                if main:
                    add_in(u - 1, 1)
                if chain:
                    k0 = dve.value_load(ktab[0:1, bass.ds(u * MC, 1)], min_val=0, max_val=KD)
                    er_k0 = er_tab[:, bass.ds(k0 * H, H)]
                    mu_v = mu.rearrange("p (c w) -> p c w", w=H + 1)
                    dve.wait_ge(s_mu, u + 1)
                    soft.done(nc.vector.tensor_scalar(absent[:, :], mu_v[:, :, H:H + 1].rearrange("p c o -> p (c o)"),
                                                      BIG, -BIG, ALU.mult, ALU.add))
                    soft.done(nc.vector.tensor_tensor(m_old[:, :], carry[:, :],
                                                      kmask[:, 0, bass.ds(u * MC, 1)].to_broadcast([P, H]), ALU.add))
                    soft.after()
                    soft.done(nc.vector.tensor_tensor(muH[:, :, :].rearrange("p h c -> p c h"), mu_v[:, :, 0:H],
                                                      absent[:, :].unsqueeze(2).to_broadcast([P, MC, H]), ALU.add))
                    soft.after()
                    soft.done(nc.vector.tensor_tensor(muH[:, :, 0], muH[:, :, 0], m_old[:, :], ALU.max))
                    dve.wait_ge(s_prep, u * 3 + 3)
                    soft.after()
                    soft.done(nc.vector.tensor_tensor_scan(upmax[:, :], kf_rep[:, :, :].rearrange("p h c -> p (h c)"),
                                                           muH[:, :, :].rearrange("p h c -> p (h c)"), -BIG,
                                                           ALU.add, ALU.max))
                    soft.after()
                    nc.vector.tensor_tensor_scan(MH[:, :, :].rearrange("p h c -> p (h c)")[:, ::-1],
                                                 kb_rep[:, :, :].rearrange("p h c -> p (h c)")[:, ::-1],
                                                 upmax[:, ::-1], -BIG, ALU.add, ALU.max).then_inc(s_MH, 1)
                    dve.wait_ge(s_MH, u + 1)
                    soft.done(nc.vector.tensor_copy(carry[:, :], MH[:, :, MC - 1]))
                    soft.done(nc.vector.tensor_tensor(fz[:, 0, :], m_old[:, :], er_k0, ALU.add))
                    soft.done(nc.vector.tensor_tensor(fz[:, 1, :], MH[:, :, 0], er_k0, ALU.add))
                    soft.after()
                    soft.done(nc.vector.scalar_tensor_tensor(out=fl[:, :, :], in0=fz[:, :, :], scalar=SLOPE, in1=fz[:, :, :],
                                                             op0=ALU.mult, op1=ALU.max))
                    soft.after()
                    nc.vector.tensor_tensor(fd[:, :], fl[:, 0, :], fl[:, 1, :], ALU.subtract).then_inc(s_fd, 1)
                if main:
                    add_in(u - 1, 2)
                if chain:
                    dve.wait_ge(s_mxe, u + 2)
                    dve.wait_ge(s_ers, u + 2)
                    soft.done(nc.vector.tensor_tensor(zz[:, 0, :].rearrange("p (c h) -> p c h", h=H), rows[:, r, :, EX:ROW],
                                                      erS[:, :].rearrange("p (c h) -> p c h", h=H), ALU.add))
                    soft.done(nc.vector.tensor_tensor(zz[:, 1, :], mx_e, erS[:, :], ALU.add))
                    soft.after()
                    soft.done(nc.vector.scalar_tensor_tensor(out=zl[:, :, :], in0=zz[:, :, :], scalar=SLOPE, in1=zz[:, :, :],
                                                             op0=ALU.mult, op1=ALU.max))
                    soft.after()
                    soft.done(nc.vector.tensor_tensor(zl[:, 0, :], zl[:, 0, :], zl[:, 1, :], ALU.subtract))
                    soft.after()
                    nc.vector.tensor_scalar(zd[:, :], zl[:, 0, :], 0.0, None, ALU.min).then_inc(s_zd, 1)
                if main:
                    add_in(u - 1, 3)
                if chain:
                    dve.wait_ge(s_fac, u + 1)
                    if main:
                        dve.wait_ge(s_fl, u * MC + 2)
                    a = acc[:, bass.ds(k0 * RS + HF, D)].rearrange("p (h d) -> p h d", d=DH)
                    soft.done(nc.vector.tensor_tensor(a, a, fac[:, :].unsqueeze(2).to_broadcast([P, H, DH]), ALU.mult))
                    a = acc[:, bass.ds(k0 * RS + EX, H)]
                    soft.done(nc.vector.tensor_tensor(a, a, fac[:, :], ALU.mult))
                    soft.after()
                    dve.wait_ge(s_ex, u + 1)
                    for q in range(Q):
                        cs = slice(q * QC, (q + 1) * QC)
                        a = rows[:, r, cs, HF:EX].rearrange("p c (h d) -> p c h d", d=DH)
                        nc.vector.tensor_tensor(a, a, rows[:, r, cs, EX:ROW].unsqueeze(3).to_broadcast([P, QC, H, DH]),
                                                ALU.mult).then_inc(s_prod, 1)
                    assert soft.n == SOFT, soft.n
                    build(u + 1, (r + 1) % RING)

            build(0, 0)
            slot(0, 0, True, False)
            with dve.Fori(0, (NM - 1) // RING) as i:
                for j in range(RING):
                    slot(i * RING + (1 + j), (1 + j) % RING, True, True)
            slot(NM, None, False, True)

            dve.wait_ge(s_fl, COLS + 2)
            EP = 20

            def rows_of(v):
                return v.unsqueeze(2).to_broadcast([P, EB, D])

            def batch(b, loaded):
                ep = Chain(dve, s_ep, b * EP)
                A = acc[:, bass.ds(b * (EB * RS), EB * RS)].rearrange("p (k w) -> p k w", w=RS)
                cnt = A[:, :, ONE:ONE + 1].rearrange("p k o -> p (k o)")
                ep.done(nc.vector.tensor_scalar(den_f, A[:, :, EX:ROW], DEN_FLOOR, None, ALU.max))
                ep.done(nc.vector.tensor_scalar(small(0), cnt, 1.0, None, ALU.max))
                ep.done(nc.vector.tensor_scalar(small(1), cnt, 1.0, None, ALU.add))
                ep.done(nc.vector.tensor_scalar(small(2), cnt, 1.0, None, ALU.min))
                ep.after()
                ep.done(nc.vector.reciprocal(rden_f, den_f))
                ep.done(nc.vector.reciprocal(small(3), small(0)))
                ep.done(nc.vector.reciprocal(small(4), small(1)))
                ep.after()
                nc.vector.tensor_tensor(es_f, A[:, :, 0:D], rows_of(small(3)), ALU.mult).then_inc(s_es, 1)
                ep.done(nc.vector.tensor_tensor(o_f.rearrange("p k (h d) -> p k h d", d=DH),
                                                A[:, :, HF:EX].rearrange("p k (h d) -> p k h d", d=DH),
                                                rden_f.unsqueeze(3).to_broadcast([P, EB, H, DH]), ALU.mult))
                dve.wait_ge(s_lx, loaded)
                ep.done(nc.vector.tensor_tensor(t_f, hf_f, rows_of(small(4)), ALU.mult))
                for other in (t_f, x_f, bias_b[:, :].unsqueeze(1).to_broadcast([P, EB, D])):
                    ep.after()
                    ep.done(nc.vector.tensor_tensor(o_f, o_f, other, ALU.add))
                ep.done(nc.vector.tensor_tensor(t_f, be_b[:, :].unsqueeze(1).to_broadcast([P, EB, D]),
                                                rows_of(small(2)), ALU.mult))
                ep.after()
                ep.done(nc.vector.tensor_tensor(o_f, o_f, t_f, ALU.add))
                dve.wait_ge(s_he, b * EB + EB)
                ep.after()
                for a, tiles in ((0, 4), (1, EB - 4)):
                    v = o_f[:, 4 * a:4 * a + tiles, :]
                    ep.done(nc.vector.tensor_tensor(v, v, ps_main[a][:, 0:tiles * P].rearrange("p (k d) -> p k d", d=D), ALU.add))
                ep.after()
                ep.done(nc.vector.tensor_reduce(small(5), o_f, AX.X, ALU.add))
                ep.after()
                ep.done(nc.vector.tensor_scalar(small(8), small(5), -1.0 / D, None, ALU.mult))
                ep.after()
                nc.vector.tensor_tensor(o_f, o_f, rows_of(small(8)), ALU.add).then_inc(s_sq, 1)
                dve.wait_ge(s_var, b + 1)
                ep.done(nc.vector.tensor_reduce(small(5), t_f, AX.X, ALU.add))
                ep.after()
                nc.vector.tensor_scalar(small(6), small(5), 1.0 / D, LN_EPS, ALU.mult, ALU.add).then_inc(s_std, 1)
                dve.wait_ge(s_rt, b + 1)
                ep.done(nc.vector.reciprocal(small(8), small(7)))
                ep.after()
                dve.wait_ge(s_sq, b + 1)
                nc.vector.tensor_tensor(o_f, o_f, rows_of(small(8)), ALU.mult).then_inc(s_o, 1)
                assert ep.n == EP, ep.n

            with dve.Fori(0, NEB - 1) as b:
                batch(b, b * 32 + 32)
                dve.wait_ge(s_out, b * 16 + 16)
            batch(NEB - 1, (NEB - 1) * 32 + 64)


def kernel(x, src, dst, edge_attr_128, L0_gnn_W_fc, L0_gnn_attn_l, L0_gnn_attn_r, L0_gnn_bias, L0_gnn_W_e, L0_gnn_b_e):
    import concourse.bacc as bacc
    from concourse.bass_utils import run_bass_kernel_spmd

    n, e = x.shape[0], src.shape[0]
    pad = -e % P
    past = -(-n // P) * P - 1
    arrays = {
        "x": x,
        "src": np.pad(np.asarray(src), (0, pad)),
        "dst": np.pad(np.asarray(dst), (0, pad), constant_values=past),
        "edge_attr": np.pad(np.asarray(edge_attr_128), ((0, pad), (0, 0))),
        "w_fc": L0_gnn_W_fc, "attn_l": L0_gnn_attn_l, "attn_r": L0_gnn_attn_r, "bias": L0_gnn_bias,
        "w_e": L0_gnn_W_e, "b_e": L0_gnn_b_e,
    }
    arrays = {k: np.ascontiguousarray(v) for k, v in arrays.items()}
    nc = bacc.Bacc("TRN2", target_bir_lowering=False, num_devices=1)
    args = [nc.dram_tensor(k, v.shape, mybir.dt.from_np(v.dtype), kind="ExternalInput").ap() for k, v in arrays.items()]
    out = nc.dram_tensor("out", x.shape, F32, kind="ExternalOutput").ap()
    gat_layer(nc, *args, out)
    return run_bass_kernel_spmd(nc, [arrays], core_ids=[0]).results[0]["out"]
```

```python
import numpy as np
import concourse.bass as bass
from concourse import mybir
from contextlib import ExitStack

F32 = mybir.dt.float32
I32 = mybir.dt.int32
BF16 = mybir.dt.bfloat16
ENG = mybir.EngineType
ALU = mybir.AluOpType
ACT = mybir.ActivationFunctionType
AX = mybir.AxisListType

P = 128
BIG = float(2.0 ** 100)
BANK = 512
DEN_FLOOR = 1e-30
LN_EPS = 1e-5
SLOPE = 0.2


def top(v):
    return v.bitcast(BF16)[..., 1::2]


class Chain:

    def __init__(self, eng, sem, base):
        self.eng, self.sem, self.base, self.n = eng, sem, base, 0

    def done(self, ins):
        ins.then_inc(self.sem, 1)
        self.n += 1

    def after(self):
        self.eng.wait_ge(self.sem, self.base + self.n)


def gat_layer(nc, x, src, dst, ef, w_fc, attn_l, attn_r, bias, w_e, b_e, out):
    N, D = x.shape
    H, DH = attn_l.shape
    EPAD = src.shape[0]
    ET = EPAD // P
    NT = -(-N // P)
    TAIL = N - (NT - 1) * P
    MC = 16
    COLS = ET + NT + (-(ET + NT)) % MC
    NM = COLS // MC
    NB = -(-COLS // P)
    CP = NB * P
    KD = NT
    RING = 3
    Q = 4
    QC = MC // Q
    ONE, HF, EX, ROW = D, D + 1, 2 * D + 1, 2 * D + 1 + H
    RS = ROW + 1
    TW = D + H
    WC = D + 2 * H
    assert NM == 1 + RING * ((NM - 1) // RING) and MC * H == P
    XC = 4
    NXC = (NT - 1) // XC
    assert NXC % 2 == 0 and NXC * XC == NT - 1
    EB = 7
    NEB = NT // EB
    assert NEB * EB == NT

    with ExitStack() as ctx:
        def sb(name, shape, dt=F32):
            return ctx.enter_context(nc.sbuf_tensor(name, shape, dt))

        def sem(name):
            return ctx.enter_context(nc.semaphore(name))

        ctx.enter_context(nc.allow_non_contiguous_dma(reason="small tables, and one column of dst"))
        node_table = nc.dram_tensor("node_table", (N, TW), F32, kind="Internal").ap()
        tk_dram = nc.dram_tensor("tk_dram", (2, CP), I32, kind="Internal").ap()

        acc = sb("acc", [P, (NT + 1) * RS])
        rows = sb("rows", [P, RING, MC, RS])
        S = sb("S", [P, RING, MC, P])
        Sb = sb("Sb", [P, RING, MC, P], BF16)
        ST = sb("ST", [P, MC, P], BF16)
        er_tab = sb("er_tab", [P, (NT + 1) * H])
        er_rest = sb("er_rest", [P, 2, (NT + 1) * H])
        er3 = sb("er3", [P, (NT + 1) * 3 * H], BF16)
        ident_b = sb("ident_b", [P, P], BF16)
        ident = sb("ident", [P, P])
        iota_row = sb("iota_row", [P, P])
        ones_row = sb("ones_row", [1, P])
        dlocT = sb("dlocT", [P, CP])
        lastT = sb("lastT", [P, CP])
        startT = sb("startT", [P, CP])
        srcT = sb("srcT", [P, CP], I32)
        kmask = sb("kmask", [P, 3, CP])
        ktab = sb("ktab", [1, CP], I32)
        ttab = sb("ttab", [1, CP], I32)
        btab = sb("btab", [1, CP], I32)
        wtab = sb("wtab", [1, CP], I32)
        zeros_b = sb("zeros_b", [P, P], BF16)
        er_now = sb("er_now", [P, MC, 3 * H], BF16)
        src_now = sb("src_now", [P, RING, MC], I32)
        start_rep = sb("start_rep", [P, MC, H])
        el_now = sb("el_now", [P, MC, H])
        startS = sb("startS", [P, P])
        runmax = sb("runmax", [P, P])
        V = sb("V", [P, MC, 3, H + 1])
        absent = sb("absent", [P, MC])
        muH = sb("muH", [P, H, MC])
        kf_rep = sb("kf_rep", [P, H, MC])
        kb_rep = sb("kb_rep", [P, H, MC])
        upmax = sb("upmax", [P, P])
        MH3 = sb("MH3", [P, 3, H, MC])
        MH = MH3[:, 0, :, :]
        carry = sb("carry", [P, H])
        m_old = sb("m_old", [P, H])
        fz = sb("fz", [P, 2, H])
        fl = sb("fl", [P, 2, H])
        fd = sb("fd", [P, H])
        fac = sb("fac", [P, H])
        erS = sb("erS", [P, P])
        zz = sb("zz", [P, 2, P])
        zl = sb("zl", [P, 2, P])
        zd = sb("zd", [P, P])
        w_sb = sb("w_sb", [P, WC])
        we_sb = sb("we_sb", [P, D])
        attn_b = sb("attn_b", [P, 2, D])
        wa = sb("wa", [P, 2, D])
        bias_b = sb("bias_b", [P, D])
        be_b = sb("be_b", [P, D])
        xin = S[:, 0, 0:2 * XC, :].rearrange("p (h c) d -> p h c d", h=2)
        xT = S[:, 1, 0:2 * XC, :].rearrange("p (h c) d -> p h c d", h=2)
        stage = S[:, 2, :, :].rearrange("p a b -> p (a b)")[:, 0:2 * XC * TW].rearrange("p (h c d) -> p h c d", h=2, c=XC)
        flat = rows[:, :, :, :].rearrange("p a b c -> p (a b c)")
        W7 = NB * P

        def piece(n, width=W7):
            return flat[:, n * W7:n * W7 + width]

        dcol_i = piece(0).bitcast(I32).rearrange("p (b e) -> p b e", e=P)
        scol_i = piece(1).bitcast(I32).rearrange("p (b e) -> p b e", e=P)
        dcol = piece(2).rearrange("p (b e) -> p b e", e=P)
        scol = piece(3).rearrange("p (b e) -> p b e", e=P)
        dloc = piece(4).rearrange("p (b e) -> p b e", e=P)
        lastc = piece(5).rearrange("p (b e) -> p b e", e=P)
        startc = piece(6).rearrange("p (b e) -> p b e", e=P)
        stb = piece(7)
        cmp_t = piece(8)
        first_i = piece(9)[0:1, :].bitcast(I32)
        tile_i = piece(10)[0:1, :].bitcast(I32)
        first_s = piece(11)[0:1, :]
        krow = flat[0:1, 12 * W7:12 * W7 + CP]
        kmrow_b = acc[0:1, 3 * CP:4 * CP]
        kmrow = acc[0:1, 0:3 * CP].rearrange("p (a c) -> p a c", a=3)
        sid_i = sb("sid_i", [P, NB], I32)
        sid = sb("sid", [P, NB])
        tcnt = sb("tcnt", [P, NB])
        kcol = sb("kcol", [P, NB])
        k128 = sb("k128", [P, NB])
        t_i = sb("t_i", [P, NB], I32)
        k_i = sb("k_i", [P, NB], I32)

        def bank(name):
            return ctx.enter_context(nc.psum_tensor(name, [P, BANK], F32))

        ps_pair = ctx.enter_context(nc.psum_tensor("ps_pair", [P, 2 * BANK], F32))
        ps_main = [ps_pair[:, 0:BANK], ps_pair[:, BANK:2 * BANK]]
        ps_st = [bank("ps_st0"), bank("ps_st1")]
        ps_x = bank("ps_x")
        ps_f = bank("ps_f")
        ps_e = bank("ps_e")
        ps_t = bank("ps_t")
        el_t, start_t = ps_x[:, 0:P], ps_x[:, P:2 * P]
        run_e, mu = ps_f[:, 0:P], ps_f[:, P:P + MC * (H + 1)]
        er_e, mx_e = ps_e[:, 0:P], ps_e[:, P:2 * P]

        s_id0, s_id, s_iota, s_one = sem("s_id0"), sem("s_id"), sem("s_iota"), sem("s_one")
        s_w, s_bias, s_first = sem("s_w"), sem("s_bias"), sem("s_first")
        s_wcat = sem("s_wcat")
        s_xz = sem("s_xz")
        s_x = [sem("s_x0"), sem("s_x1")]
        s_xt, s_xtc, s_hf, s_hfc = sem("s_xt"), sem("s_xtc"), sem("s_hf"), sem("s_hfc")
        s_er = sem("s_er")
        s_tab = [sem("s_tab0"), sem("s_tab1")]
        s_pre = sem("s_pre")
        s_stb, s_stbc = sem("s_stb"), sem("s_stbc")
        s_ti, s_dg, s_sg, s_tk, s_tkr = sem("s_ti"), sem("s_dg"), sem("s_sg"), sem("s_tk"), sem("s_tkr")
        s_cols = sem("s_cols")
        s_tt, s_ttc = sem("s_tt"), sem("s_ttc")
        s_kmr, s_km, s_kmc = sem("s_kmr"), sem("s_km"), sem("s_kmc")
        s_init = sem("s_init")
        s_idx, s_tick = sem("s_idx"), sem("s_tick")
        s_g = [sem(f"s_g{r}") for r in range(RING)]
        s_ef = [sem(f"s_ef{r}") for r in range(RING)]
        s_prep, s_S, s_Sf = sem("s_prep"), sem("s_S"), sem("s_Sf")
        s_stp, s_st = sem("s_stp"), sem("s_st")
        s_ere, s_ers = sem("s_ere"), sem("s_ers")
        s_elc, s_ern = sem("s_elc"), sem("s_ern")
        s_elt, s_starts, s_run, s_rune = sem("s_elt"), sem("s_starts"), sem("s_run"), sem("s_rune")
        s_V, s_mu, s_MH, s_mxe = sem("s_V"), sem("s_mu"), sem("s_MH"), sem("s_mxe")
        s_fd, s_fac, s_zd, s_ex, s_prod = sem("s_fd"), sem("s_fac"), sem("s_zd"), sem("s_ex"), sem("s_prod")
        s_soft = sem("s_soft")
        s_mm, s_fl = sem("s_mm"), sem("s_fl")
        s_lx, s_ep = sem("s_lx"), sem("s_ep")
        s_es, s_est, s_estc, s_he, s_o, s_out = sem("s_es"), sem("s_est"), sem("s_estc"), sem("s_he"), sem("s_o"), sem("s_out")
        s_sq, s_var, s_std, s_rt = sem("s_sq"), sem("s_var"), sem("s_std"), sem("s_rt")
        block = ctx.enter_context(nc.Block())

        def fin(n):
            return flat[:, n * EB * D:(n + 1) * EB * D].rearrange("p (k d) -> p k d", d=D)

        x_f, hf_f, es_f, o_f, t_f = fin(0), fin(1), fin(2), fin(3), fin(4)
        esT_f = fin(5)
        sm = flat[:, 6 * EB * D:6 * EB * D + 128]

        def small(n):
            return sm[:, n * EB:(n + 1) * EB]

        den_f = flat[:, 6 * EB * D + 128:6 * EB * D + 128 + EB * H].rearrange("p (k h) -> p k h", h=H)
        rden_f = flat[:, 6 * EB * D + 256:6 * EB * D + 256 + EB * H].rearrange("p (k h) -> p k h", h=H)

        def columns(engine, table, m, n, most):
            return nc.values_load_multi_w_load_instructions(table[0:1, bass.ds(m * MC, n)], engines=(engine,),
                                                            min_val=0, max_val=most)[1]

        G16 = MC * 16

        @block.sync
        def _(sp):
            sp.dma_start(w_sb[:, 0:D], w_fc[:, :]).then_inc(s_w, 16)
            sp.dma_start(attn_b[:, 0, :], attn_l.rearrange("h d -> (h d)").partition_broadcast(P)).then_inc(s_w, 16)
            sp.dma_start(attn_b[:, 1, :], attn_r.rearrange("h d -> (h d)").partition_broadcast(P)).then_inc(s_w, 16)
            sp.dma_start(first_i[:, 0:ET], dst.rearrange("(a t e) -> a t e", a=1, e=P)[:, :, 0]).then_inc(s_first, 16)
            def load_x(c, h):
                sp.dma_start(xin[:, h, :, :],
                             x[bass.ds(c * (XC * P), XC * P), :].rearrange("(k p) d -> p k d", p=P)).then_inc(s_x[h], 16)

            def store_table(c, h):
                sp.wait_ge(s_er, (c + 1) * 2)
                sp.dma_start(node_table[bass.ds(c * (XC * P), XC * P), :].rearrange("(k p) w -> p k w", p=P),
                             stage[:, h, :, :]).then_inc(s_tab[h], 16)

            load_x(0, 0)
            load_x(1, 1)
            with sp.Fori(0, NXC // 2 - 1) as i:
                for h in range(2):
                    store_table(i * 2 + h, h)
                    load_x(i * 2 + (h + 2), h)
            for h in range(2):
                store_table(NXC - 2 + h, h)
            sp.wait_ge(s_xz, 1)
            sp.dma_start(xin[0:TAIL, 0, 0, :], x[NXC * XC * P:N, :]).then_inc(s_x[0], 16)
            sp.wait_ge(s_er, NXC * 2 + 1)
            sp.dma_start(node_table[NXC * XC * P:N, :], stage[0:TAIL, 0, 0, :]).then_inc(s_tab[0], 16)
            sp.dma_start(we_sb[:, :], w_e[:, :]).then_inc(s_bias, 16)
            sp.dma_start(bias_b[:, :], bias.partition_broadcast(P)).then_inc(s_bias, 16)
            sp.dma_start(be_b[:, :], b_e.partition_broadcast(P)).then_inc(s_bias, 16)
            sp.wait_ge(s_ti, 1)
            sp.dma_start(tk_dram[0, :].rearrange("(b p) -> p b", p=P), t_i[:, :]).then_inc(s_tk, 16)
            sp.dma_start(tk_dram[1, :].rearrange("(b p) -> p b", p=P), k_i[:, :]).then_inc(s_tk, 16)
            sp.wait_ge(s_tk, 32)
            sp.dma_start(ttab[:, :], tk_dram[0:1, :]).then_inc(s_tkr, 16)
            sp.dma_start(ktab[:, :], tk_dram[1:2, :]).then_inc(s_tkr, 16)
            sp.wait_ge(s_tkr, 32)
            sp.wait_ge(s_init, 1)

            def load_ef(m, r, first):
                ts = columns(ENG.SP, ttab, m, MC, ET - 1)
                for q in range(Q):
                    if not first:
                        sp.wait_ge(s_mm, (m - RING) * MC + (q + 1) * QC)
                    for c in range(q * QC, (q + 1) * QC):
                        sp.dma_start(rows[:, r, c, 0:D], ef[bass.ds(ts[c] * P, P), :]).then_inc(s_ef[r], 16)

            for m in range(RING + 1):
                load_ef(m, m % RING, m < RING)
            with sp.Fori(0, (NM - 1 - RING) // RING) as i:
                for j in range(RING):
                    load_ef(i * RING + (RING + 1 + j), (1 + j) % RING, False)
            def load_fin(b, whole):
                for buf, table in ((x_f, x), (hf_f, node_table)):
                    if whole:
                        sp.dma_start(buf[:, :, :], table[bass.ds(b * (EB * P), EB * P), 0:D]
                                     .rearrange("(k p) d -> p k d", p=P)).then_inc(s_lx, 16)
                    else:
                        sp.dma_start(buf[:, 0:EB - 1, :], table[b * EB * P:(NT - 1) * P, 0:D]
                                     .rearrange("(k p) d -> p k d", p=P)).then_inc(s_lx, 16)
                        sp.dma_start(buf[0:TAIL, EB - 1, :], table[(NT - 1) * P:N, 0:D]).then_inc(s_lx, 16)

            sp.wait_ge(s_fl, COLS + 1)
            load_fin(0, True)

            def store_fin(b):
                sp.wait_ge(s_o, b + 1)
                sp.dma_start(out[bass.ds(b * (EB * P), EB * P), :].rearrange("(k p) d -> p k d", p=P),
                             o_f[:, :, :]).then_inc(s_out, 16)

            with sp.Fori(0, NEB - 2) as b:
                store_fin(b)
                load_fin(b + 1, True)
            store_fin(NEB - 2)
            load_fin(NEB - 1, False)
            sp.wait_ge(s_o, NEB)
            sp.dma_start(out[(NEB - 1) * EB * P:(NT - 1) * P, :].rearrange("(k p) d -> p k d", p=P),
                         o_f[:, 0:EB - 1, :]).then_inc(s_out, 16)
            sp.dma_start(out[(NT - 1) * P:N, :], o_f[0:TAIL, EB - 1, :]).then_inc(s_out, 16)
            sp.wait_ge(s_out, (NEB + 1) * 16)

        @block.gpsimd
        def _(pool):
            nc.gpsimd.memset(ident[:, :], 0.0).then_inc(s_id0, 1)
            pool.wait_ge(s_id0, 1)
            nc.gpsimd.affine_select(out=ident[:, :], in_=ident[:, :], compare_op=ALU.not_equal, fill=1.0, base=0,
                                    pattern=[[-1, P]], channel_multiplier=1).then_inc(s_id, 1)
            nc.gpsimd.iota(iota_row[:, :], [[1, P]], base=0, channel_multiplier=0,
                           allow_small_or_imprecise_dtypes=True).then_inc(s_iota, 1)
            nc.gpsimd.iota(tile_i[:, :], [[1, CP]], base=0, channel_multiplier=0).then_inc(s_iota, 1)
            nc.gpsimd.iota(sid_i[:, :], [[P, NB]], base=0, channel_multiplier=1).then_inc(s_iota, 1)
            pool.wait_ge(s_ti, 1)
            for b in range(NB):
                for table, into, s in ((dst, dcol_i, s_dg), (src, scol_i, s_sg)):
                    nc.gpsimd.indirect_dma_start(
                        out=into[:, b, :], out_offset=None, in_=table.rearrange("(t e) -> t e", e=P),
                        in_offset=bass.IndirectOffsetOnAxis(ap=t_i[:, b:b + 1], axis=0)).then_inc(s, 16)
            pool.wait_ge(s_ttc, 4 * NB)
            pool.wait_ge(s_init, 1)
            pool.wait_ge(s_tab[0], (NXC // 2 + 1) * 16)
            pool.wait_ge(s_tab[1], (NXC // 2) * 16)

            def gather(m, r, first):
                for q in range(Q):
                    if not first:
                        pool.wait_ge(s_mm, (m - RING) * MC + (q + 1) * QC)
                        pool.sem_inc(s_tick, 1)
                    if q == 0:
                        nc.gpsimd.tensor_copy(src_now[:, r, :], srcT[:, bass.ds(m * MC, MC)]).then_inc(s_idx, 1)
                        pool.wait_ge(s_idx, m + 1)
                        pool.sem_inc(s_tick, 1)
                    for c in range(q * QC, (q + 1) * QC):
                        nc.gpsimd.indirect_dma_start(
                            out=rows[:, r, c, HF:ROW], out_offset=None, in_=node_table[:, :],
                            in_offset=bass.IndirectOffsetOnAxis(ap=src_now[:, r, c:c + 1], axis=0)).then_inc(s_g[r], 16)

            for m in range(RING + 1):
                gather(m, m % RING, m < RING)
            with pool.Fori(0, (NM - 1 - RING) // RING) as i:
                for j in range(RING):
                    gather(i * RING + (RING + 1 + j), (1 + j) % RING, False)

        @block.tensor
        def _(pe):
            pe.wait_ge(s_id, 1)
            pe.wait_ge(s_one, 1)
            pe.wait_ge(s_wcat, 1)

            def project(c, h, tiles):
                for a in range(tiles):
                    last = nc.tensor.transpose(ps_st[h][:, a * P:(a + 1) * P], xin[:, h, a, :], ident[:, :])
                    last.then_inc(s_xt, 1)
                pe.wait_ge(s_xtc, c + 1)
                for a in range(tiles):
                    if a % 2 == 0:
                        pe.wait_ge(s_hfc, c * 2 + a // 2 + 1)
                    o = ps_main[a // 2][:, (a % 2) * WC:(a % 2) * WC + WC]
                    nc.tensor.matmul(o, xT[:, h, a, :], w_sb[:, 0:WC], start=True, stop=True).then_inc(s_hf, 1)

            with pe.Fori(0, NXC // 2) as i:
                for h in range(2):
                    pe.wait_ge(s_x[h], i * 16 + 16)
                    project(i * 2 + h, h, XC)
            pe.wait_ge(s_x[0], (NXC // 2 + 1) * 16)
            project(NXC, 0, 1)
            pe.wait_ge(s_stb, 1)
            nc.tensor.matmul(ps_x[:, 0:ET // 2], ones_row[:, :], first_s[:, 0:ET // 2], start=True, stop=True)
            nc.tensor.matmul(ps_f[:, 0:ET // 2], ones_row[:, :], first_s[:, ET // 2:2 * (ET // 2)],
                             start=True, stop=True).then_inc(s_stbc, 1)
            pe.wait_ge(s_cols, 1)
            n = 0
            for b in range(NB):
                for table in (dloc, lastc, startc, scol):
                    if n >= 1:
                        pe.wait_ge(s_ttc, n)
                    nc.tensor.transpose(ps_t[:, 0:P], table[:, b, :], ident[:, :]).then_inc(s_tt, 1)
                    n += 1
            pe.wait_ge(s_kmr, 1)
            half = CP // 2
            for a in range(3):
                for j in range(2):
                    n = a * 2 + j
                    if n >= 2:
                        pe.wait_ge(s_kmc, n - 1)
                    nc.tensor.matmul(ps_main[n % 2][:, 0:half], ones_row[:, :], kmrow[:, a, j * half:(j + 1) * half],
                                     start=True, stop=True).then_inc(s_km, 1)
            pe.wait_ge(s_init, 1)

            def exact(o, one_hot, parts):
                for s, part in enumerate(parts):
                    last = nc.tensor.matmul(o, one_hot, part, start=s == 0, stop=s == 2)
                return last

            def prepare(m, r):
                pe.wait_ge(s_S, m + 1)
                for h in range(2):
                    pe.wait_ge(s_st, m * 2 + h + 1)
                    for a in range(MC // 2):
                        last = nc.tensor.transpose(ps_st[h][:, :].bitcast(BF16)[:, a * P:(a + 1) * P],
                                                   Sb[:, r, h * (MC // 2) + a, :], ident_b[:, :])
                    last.then_inc(s_stp, 1)
                pe.wait_ge(s_st, m * 2 + 4)
                pe.wait_ge(s_ers, m + 1)
                pe.wait_ge(s_ern, m * MC + MC)
                for c in range(MC):
                    last = exact(er_e[:, c * H:(c + 1) * H], ST[:, c, :],
                                 [er_now[:, c, s * H:(s + 1) * H] for s in range(3)])
                last.then_inc(s_ere, 1)

            def slot(u, r, rm, round_m, chain, main):
                if main:
                    banks = columns(ENG.PE, btab, u - 1, MC, 1)
                    wide = columns(ENG.PE, wtab, u - 1, 1, KD)[0]
                if main:
                    main_q(u - 1, rm, round_m, 0, banks, wide)
                if chain:
                    pe.wait_ge(s_prep, u * 3 + 3)
                    nc.tensor.transpose(start_t, start_rep[:, :, :].rearrange("p c h -> p (c h)"), ident[:, :])
                    pe.wait_ge(s_elc, u + 1)
                    nc.tensor.transpose(el_t, el_now[:, :, :].rearrange("p c h -> p (c h)"), ident[:, :]).then_inc(s_elt, 1)
                if main:
                    main_q(u - 1, rm, round_m, 1, banks, wide)
                if chain:
                    pe.wait_ge(s_run, u + 1)
                    nc.tensor.transpose(run_e, runmax[:, :], ident[:, :]).then_inc(s_rune, 1)
                if main:
                    main_q(u - 1, rm, round_m, 2, banks, wide)
                if chain:
                    pe.wait_ge(s_V, u + 1)
                    for c in range(MC):
                        last = exact(mu[:, c * (H + 1):(c + 1) * (H + 1)], Sb[:, r, c, :],
                                     [top(V[:, c, s, :]) for s in range(3)])
                    last.then_inc(s_mu, 1)
                if main:
                    main_q(u - 1, rm, round_m, 3, banks, wide)
                if chain:
                    pe.wait_ge(s_MH, u + 1)
                    for c in range(MC):
                        last = exact(mx_e[:, c * H:(c + 1) * H], ST[:, c, :],
                                     [top(MH3[:, s, :, :])[:, :, c] for s in range(3)])
                    last.then_inc(s_mxe, 1)
                    prepare(u + 1, (r + 1) % RING)

            def main_q(m, r, round_m, q, banks, wide):
                if q == 0:
                    pe.wait_ge(s_ef[r], round_m)
                    pe.wait_ge(s_Sf, m + 1)
                    pe.wait_ge(s_fl, m * MC + 1)
                pe.wait_ge(s_prod, m * Q + q + 1)
                cs = range(q * QC, (q + 1) * QC)
                with pe.If(wide < 2):
                    for c in cs:
                        if c == 0:
                            nc.tensor.matmul(ps_main[1][:, 0:ROW], zeros_b[:, :], Sb[:, r, 0:3, :]
                                             .rearrange("p c n -> p (c n)")[:, 0:ROW], start=True, stop=False,
                                             skip_group_check=True)
                            o = ps_main[0][:, 0:ROW]
                        else:
                            o = ps_pair[:, bass.ds(banks[c] * BANK, ROW)]
                        nc.tensor.matmul(o, S[:, r, c, :], rows[:, r, c, 0:ROW], start=c == 0, stop=True,
                                         skip_group_check=True).then_inc(s_mm, 1)
                with pe.Else():
                    for c in cs:
                        if c > 0:
                            pe.wait_ge(s_fl, m * MC + (c + 1))
                        nc.tensor.matmul(ps_main[0][:, 0:ROW], S[:, r, c, :], rows[:, r, c, 0:ROW],
                                         start=True, stop=True, skip_group_check=True).then_inc(s_mm, 1)

            prepare(0, 0)
            slot(0, 0, None, None, True, False)
            with pe.Fori(0, (NM - 1) // RING) as i:
                for j in range(RING):
                    slot(i * RING + (1 + j), (1 + j) % RING, j, i * G16 + G16, True, True)
            slot(NM, None, (NM - 1) % RING, ((NM - 1) // RING + 1) * G16, False, True)

            pe.wait_ge(s_bias, 48)

            def edge_part(b):
                pe.wait_ge(s_es, b + 1)
                for a in range(EB):
                    nc.tensor.transpose(ps_st[a // 4][:, (a % 4) * P:(a % 4 + 1) * P], es_f[:, a, :],
                                        ident[:, :]).then_inc(s_est, 1)
                pe.wait_ge(s_estc, 2 * b + 2)
                for a in range(EB):
                    nc.tensor.matmul(ps_main[a // 4][:, (a % 4) * P:(a % 4 + 1) * P], esT_f[:, a, :], we_sb[:, :],
                                     start=True, stop=True).then_inc(s_he, 1)

            with pe.Fori(0, NEB) as b:
                edge_part(b)

        @block.scalar
        def _(act):
            def table_rows(c, h, tiles):
                act.wait_ge(s_xt, c * XC + tiles)
                nc.scalar.activation(xT[:, h, 0:tiles, :].rearrange("p k d -> p (k d)"),
                                     ps_st[h][:, 0:tiles * P], ACT.Copy).then_inc(s_xtc, 1)

            with act.Fori(0, NXC // 2) as i:
                for h in range(2):
                    table_rows(i * 2 + h, h, XC)
            table_rows(NXC, 0, 1)
            n = 0
            for b in range(NB):
                for table in (dlocT, lastT, startT, srcT):
                    act.wait_ge(s_tt, n + 1)
                    nc.scalar.activation(table[:, b * P:(b + 1) * P], ps_t[:, 0:P], ACT.Copy).then_inc(s_ttc, 1)
                    n += 1
            half = CP // 2
            for a in range(3):
                for j in range(2):
                    n = a * 2 + j
                    act.wait_ge(s_km, n + 1)
                    nc.scalar.activation(kmask[:, a, j * half:(j + 1) * half], ps_main[n % 2][:, 0:half],
                                         ACT.Copy).then_inc(s_kmc, 1)

            act.wait_ge(s_init, 1)
            act.sem_inc(s_st, 2)
            act.sem_inc(s_ers, 1)

            def prepare(m):
                act.wait_ge(s_mxe, m + 1)
                for h in range(2):
                    act.wait_ge(s_stp, m * 2 + h + 1)
                    nc.scalar.activation(ST[:, h * (MC // 2):(h + 1) * (MC // 2), :].rearrange("p c n -> p (c n)"),
                                         ps_st[h][:, :].bitcast(BF16), ACT.Copy).then_inc(s_st, 1)
                act.wait_ge(s_ere, m + 1)
                act.wait_ge(s_zd, m + 1)
                nc.scalar.activation(erS[:, :], er_e, ACT.Copy).then_inc(s_ers, 1)

            def stage_er(m):
                ks = columns(ENG.Activation, ktab, m, MC, KD)
                for c in range(MC):
                    nc.scalar.activation(er_now[:, c, :], er3[:, bass.ds(ks[c] * (3 * H), 3 * H)], ACT.Copy).then_inc(s_ern, 1)

            def softmax(m, r, round_g):
                act.wait_ge(s_g[r], round_g)
                nc.scalar.activation(el_now[:, :, :], rows[:, r, :, EX:ROW], ACT.Copy).then_inc(s_elc, 1)
                act.wait_ge(s_elt, m + 1)
                nc.scalar.activation(startS[:, :], start_t, ACT.Copy).then_inc(s_starts, 1)
                act.wait_ge(s_fd, m + 1)
                nc.scalar.activation(fac[:, :], fd[:, :], ACT.Exp).then_inc(s_fac, 1)
                act.wait_ge(s_zd, m + 2)
                nc.scalar.activation(rows[:, r, :, EX:ROW], zd[:, :].rearrange("p (c h) -> p c h", h=H),
                                     ACT.Exp).then_inc(s_ex, 1)

            def widen(m, r):
                act.wait_ge(s_S, m + 1)
                nc.scalar.activation(S[:, r, :, :], Sb[:, r, :, :], ACT.Copy).then_inc(s_Sf, 1)

            act.sem_inc(s_mxe, 1)
            widen(0, 0)
            stage_er(0)
            prepare(0)
            softmax(0, 0, G16)
            widen(1, 1)
            stage_er(1)
            prepare(1)
            with act.Fori(0, (NM - 1) // RING) as i:
                for j in range(RING):
                    softmax(i * RING + (1 + j), (1 + j) % RING, i * G16 + (1 + (1 + j) // RING) * G16)
                    widen(i * RING + (2 + j), (2 + j) % RING)
                    stage_er(i * RING + (2 + j))
                    prepare(i * RING + (2 + j))

            def last_stage(b):
                for a, tiles in ((0, 4), (1, EB - 4)):
                    act.wait_ge(s_est, b * EB + (4 if a == 0 else EB))
                    nc.scalar.activation(esT_f[:, 4 * a:4 * a + tiles, :].rearrange("p k d -> p (k d)"),
                                         ps_st[a][:, 0:tiles * P], ACT.Copy).then_inc(s_estc, 1)
                act.wait_ge(s_sq, b + 1)
                nc.scalar.activation(t_f[:, :, :], o_f[:, :, :], ACT.Square).then_inc(s_var, 1)
                act.wait_ge(s_std, b + 1)
                nc.scalar.activation(small(7), small(6), ACT.Sqrt).then_inc(s_rt, 1)

            with act.Fori(0, NEB) as b:
                last_stage(b)

        @block.vector
        def _(dve):
            pre = Chain(dve, s_pre, 0)
            nc.vector.memset(ones_row[:, :], 1.0).then_inc(s_one, 1)
            dve.wait_ge(s_w, 48)
            for a in range(2):
                pre.done(nc.vector.tensor_tensor(wa[:, a, :], w_sb[:, 0:D], attn_b[:, a, :], ALU.mult))
            pre.after()
            nc.vector.tensor_reduce(w_sb[:, D:WC].rearrange("p (a h) -> p a h", h=H),
                                    wa[:, :, :].rearrange("p a (h d) -> p a h d", d=DH),
                                    AX.X, ALU.add).then_inc(s_wcat, 1)
            dve.wait_ge(s_first, 16)
            dve.wait_ge(s_iota, 3)
            pre.done(nc.vector.tensor_single_scalar(first_i[:, 0:ET], first_i[:, 0:ET], P.bit_length() - 1,
                                                    ALU.arith_shift_right))
            pre.after()
            nc.vector.tensor_tensor(first_s[:, 0:ET], first_i[:, 0:ET], tile_i[:, 0:ET], ALU.add).then_inc(s_stb, 1)
            pre.done(nc.vector.tensor_copy(sid[:, :], sid_i[:, :]))

            pre.done(nc.vector.memset(er_tab[:, NT * H:(NT + 1) * H], 0.0))
            dve.sem_inc(s_hfc, 2)

            def results(c, h, tiles):
                for g in range(-(-tiles // 2)):
                    k = min(2, tiles - 2 * g)
                    dve.wait_ge(s_hf, c * XC + 2 * g + k)
                    v = ps_main[g][:, 0:k * WC].rearrange("p (k w) -> p k w", w=WC)
                    nc.vector.tensor_copy(stage[:, h, 2 * g:2 * g + k, :], v[:, :, 0:TW]).then_inc(s_er, 1)
                    nc.vector.tensor_scalar(er_tab[:, bass.ds((c * XC + 2 * g) * H, k * H)]
                                            .rearrange("p (k h) -> p k h", h=H), v[:, :, TW:WC], 1.0, None,
                                            ALU.mult).then_inc(s_hfc, 1)

            for h in range(2):
                results(h, h, XC)
            with dve.Fori(1, NXC // 2) as i:
                for h in range(2):
                    dve.wait_ge(s_tab[h], i * 16)
                    results(i * 2 + h, h, XC)
            dve.wait_ge(s_xt, NXC * XC)
            nc.vector.memset(xin[:, 0, 0, :], 0.0).then_inc(s_xz, 1)
            dve.wait_ge(s_tab[0], NXC // 2 * 16)
            results(NXC, 0, 1)

            pre.after()
            dve.wait_ge(s_hfc, NXC * 2 + 3)
            pre.done(nc.vector.tensor_tensor(er_rest[:, 0, :], er_tab[:, :], top(er_tab[:, :]), ALU.subtract))
            pre.after()
            pre.done(nc.vector.tensor_tensor(er_rest[:, 1, :], er_rest[:, 0, :], top(er_rest[:, 0, :]), ALU.subtract))
            pre.after()
            for s, part in enumerate((er_tab[:, :], er_rest[:, 0, :], er_rest[:, 1, :])):
                pre.done(nc.vector.tensor_copy(er3[:, :].rearrange("p (k s h) -> p k s h", s=3, h=H)[:, :, s, :],
                                               top(part).rearrange("p (k h) -> p k h", h=H)))
            dve.wait_ge(s_id, 1)
            pre.done(nc.vector.tensor_copy(ident_b[:, :], ident[:, :]))
            pre.done(nc.vector.memset(zeros_b[:, :], 0.0))

            dve.wait_ge(s_stbc, 1)
            for j, p_ in enumerate((ps_x, ps_f)):
                pre.done(nc.vector.tensor_copy(stb[:, j * (ET // 2):(j + 1) * (ET // 2)], p_[:, 0:ET // 2]))
            for b in range(NB):
                pre.after()
                pre.done(nc.vector.tensor_scalar(cmp_t[:, 1:ET], stb[:, 1:ET], sid[:, b:b + 1], None, ALU.is_le))
                pre.after()
                pre.done(nc.vector.tensor_reduce(tcnt[:, b:b + 1], cmp_t[:, 1:ET], AX.X, ALU.add))
            pre.after()
            pre.done(nc.vector.tensor_tensor(kcol[:, :], sid[:, :], tcnt[:, :], ALU.subtract))
            pre.after()
            pre.done(nc.vector.tensor_scalar(kcol[:, :], kcol[:, :], float(KD), None, ALU.min))
            pre.done(nc.vector.tensor_copy(t_i[:, :], tcnt[:, :]))
            pre.after()
            pre.done(nc.vector.tensor_scalar(k128[:, :], kcol[:, :], float(P), None, ALU.mult))
            pre.done(nc.vector.tensor_copy(k_i[:, :], kcol[:, :]))
            pre.after()
            dve.sem_inc(s_ti, 1)

            dve.wait_ge(s_dg, NB * 16)
            pre.done(nc.vector.tensor_copy(dcol, dcol_i))
            dve.wait_ge(s_sg, NB * 16)
            pre.done(nc.vector.tensor_copy(scol, scol_i))
            pre.after()
            pre.done(nc.vector.tensor_tensor(dloc, dcol, k128[:, :].unsqueeze(2).to_broadcast([P, NB, P]), ALU.subtract))
            pre.done(nc.vector.tensor_tensor(lastc[:, :, 0:P - 1], dcol[:, :, 0:P - 1], dcol[:, :, 1:P], ALU.not_equal))
            pre.done(nc.vector.memset(lastc[:, :, P - 1:P], 1.0))
            pre.after()
            pre.done(nc.vector.tensor_scalar(startc[:, :, 1:P], lastc[:, :, 0:P - 1], -BIG, None, ALU.mult))
            pre.done(nc.vector.memset(startc[:, :, 0:1], -BIG))
            pre.after()
            dve.sem_inc(s_cols, 1)

            dve.wait_ge(s_tkr, 32)
            pre.done(nc.vector.tensor_copy(krow, ktab[:, :]))
            pre.after()
            pre.done(nc.vector.tensor_tensor(kmrow[:, 0, 1:CP], krow[:, 1:CP], krow[:, 0:CP - 1], ALU.not_equal))
            pre.done(nc.vector.memset(kmrow[:, 0, 0:1], 1.0))
            pre.after()
            pre.done(nc.vector.tensor_scalar(kmrow[:, 1, :], kmrow[:, 0, :], -BIG, None, ALU.mult))
            pre.done(nc.vector.tensor_scalar(kmrow[:, 2, 0:CP - 1], kmrow[:, 0, 1:CP], -BIG, None, ALU.mult))
            pre.after()
            pre.done(nc.vector.tensor_copy(kmrow[:, 0, :], kmrow[:, 1, :]))
            pre.after()
            by_macro = kmrow.rearrange("p a (m c) -> p a m c", c=MC)
            pre.done(nc.vector.memset(by_macro[:, 1, :, 0:1], -BIG))
            pre.done(nc.vector.memset(by_macro[:, 2, :, MC - 1:MC], -BIG))
            pre.after()
            dve.sem_inc(s_kmr, 1)
            k_mac = krow.rearrange("p (m c) -> p m c", c=MC)
            b_mac = kmrow_b.rearrange("p (m c) -> p m c", c=MC)
            k_first = k_mac[:, :, 0:1].to_broadcast([1, CP // MC, MC])
            pre.done(nc.vector.tensor_tensor(b_mac, k_mac, k_first, ALU.subtract))
            pre.after()
            pre.done(nc.vector.tensor_copy(wtab[:, :].rearrange("p (m c) -> p m c", c=MC),
                                           b_mac[:, :, MC - 1:MC].to_broadcast([1, CP // MC, MC])))
            pre.done(nc.vector.tensor_scalar(btab[:, :], kmrow_b, 1.0, None, ALU.min))

            dve.wait_ge(s_ttc, 4 * NB)
            dve.wait_ge(s_kmc, 6)
            dve.wait_ge(s_tab[0], (NXC // 2 + 1) * 16)
            dve.wait_ge(s_tab[1], NXC // 2 * 16)
            pre.after()
            pre.done(nc.vector.memset(acc[:, :], 0.0))
            pre.done(nc.vector.memset(rows[:, :, :, ONE:ONE + 1], 1.0))
            pre.done(nc.vector.memset(carry[:, :], -BIG))
            pre.after()
            dve.sem_inc(s_init, 1)
            dve.sem_inc(s_fl, 1)
            dve.sem_inc(s_zd, 1)

            def masks(m):
                cols = bass.ds(m * MC, MC)
                for rep_, table in ((kf_rep, kmask[:, 1, cols]), (kb_rep, kmask[:, 2, cols])):
                    nc.vector.tensor_scalar(rep_[:, :, :], table.unsqueeze(1).to_broadcast([P, H, MC]), 1.0, None,
                                            ALU.mult).then_inc(s_prep, 1)
                nc.vector.tensor_scalar(start_rep[:, :, :], startT[:, cols].unsqueeze(2).to_broadcast([P, MC, H]), 1.0,
                                        None, ALU.mult).then_inc(s_prep, 1)

            def build(m, r):
                cols = bass.ds(m * MC, MC)
                nc.vector.tensor_tensor(Sb[:, r, :, :], iota_row[:, :].unsqueeze(1).to_broadcast([P, MC, P]),
                                        dlocT[:, cols].unsqueeze(2).to_broadcast([P, MC, P]),
                                        ALU.is_equal).then_inc(s_S, 1)

            def add_in(m, ks):
                def add(k, bank_):
                    a = acc[:, bass.ds(k * RS, ROW)]
                    return nc.vector.tensor_tensor(a, a, ps_main[bank_][:, 0:ROW], ALU.add)

                with dve.If(ks[MC - 1] - ks[0] < 2):
                    dve.wait_ge(s_mm, m * MC + MC)
                    add(ks[0], 0).then_inc(s_fl, MC // 2)
                    dve.wait_ge(s_fl, m * MC + (MC // 2 + 1))
                    add(ks[MC - 1], 1).then_inc(s_fl, MC // 2)
                with dve.Else():
                    for c in range(MC):
                        dve.wait_ge(s_mm, m * MC + (c + 1))
                        dve.wait_ge(s_fl, m * MC + (c + 1))
                        add(ks[c], 0).then_inc(s_fl, 1)

            SOFT = 20

            def slot(u, r, chain, main):
                ks = columns(ENG.DVE, ktab, u - 1, MC + 1, KD) if main and chain else \
                    columns(ENG.DVE, ktab, u - (1 if main else 0), MC, KD)
                k0 = ks[-1] if main else ks[0]
                if chain:
                    cols = bass.ds(u * MC, MC)
                    soft = Chain(dve, s_soft, u * SOFT)
                    dve.wait_ge(s_starts, u + 1)
                    nc.vector.tensor_tensor_scan(runmax[:, :], startS[:, :], el_t, -BIG, ALU.add, ALU.max).then_inc(s_run, 1)
                if chain:
                    last = lastT[:, cols].unsqueeze(2)
                    dve.wait_ge(s_rune, u + 1)
                    soft.done(nc.vector.tensor_tensor(V[:, :, 0, 0:H], run_e.rearrange("p (c h) -> p c h", h=H),
                                                      last.to_broadcast([P, MC, H]), ALU.mult))
                    soft.done(nc.vector.tensor_scalar(V[:, :, 0, H:H + 1], last, 1.0, None, ALU.mult))
                    soft.after()
                    soft.done(nc.vector.tensor_tensor(V[:, :, 1, :], V[:, :, 0, :], top(V[:, :, 0, :]), ALU.subtract))
                    soft.after()
                    nc.vector.tensor_tensor(V[:, :, 2, :], V[:, :, 1, :], top(V[:, :, 1, :]), ALU.subtract).then_inc(s_V, 1)
                    build(u + 1, (r + 1) % RING)
                if chain:
                    er_k0 = er_tab[:, bass.ds(k0 * H, H)]
                    mu_v = mu.rearrange("p (c w) -> p c w", w=H + 1)
                    dve.wait_ge(s_mu, u + 1)
                    soft.done(nc.vector.tensor_scalar(absent[:, :], mu_v[:, :, H:H + 1].rearrange("p c o -> p (c o)"),
                                                      BIG, -BIG, ALU.mult, ALU.add))
                    soft.done(nc.vector.tensor_tensor(m_old[:, :], carry[:, :],
                                                      kmask[:, 0, bass.ds(u * MC, 1)].to_broadcast([P, H]), ALU.add))
                    soft.after()
                    soft.done(nc.vector.tensor_tensor(muH[:, :, :].rearrange("p h c -> p c h"), mu_v[:, :, 0:H],
                                                      absent[:, :].unsqueeze(2).to_broadcast([P, MC, H]), ALU.add))
                    soft.after()
                    soft.done(nc.vector.tensor_tensor(muH[:, :, 0], muH[:, :, 0], m_old[:, :], ALU.max))
                    dve.wait_ge(s_prep, u * 3 + 3)
                    soft.after()
                    soft.done(nc.vector.tensor_tensor_scan(upmax[:, :], kf_rep[:, :, :].rearrange("p h c -> p (h c)"),
                                                           muH[:, :, :].rearrange("p h c -> p (h c)"), -BIG,
                                                           ALU.add, ALU.max))
                    soft.after()
                    soft.done(nc.vector.tensor_tensor_scan(MH.rearrange("p h c -> p (h c)")[:, ::-1],
                                                           kb_rep[:, :, :].rearrange("p h c -> p (h c)")[:, ::-1],
                                                           upmax[:, ::-1], -BIG, ALU.add, ALU.max))
                    soft.after()
                    soft.done(nc.vector.tensor_tensor(MH3[:, 1, :, :], MH, top(MH), ALU.subtract))
                    soft.after()
                    nc.vector.tensor_tensor(MH3[:, 2, :, :], MH3[:, 1, :, :], top(MH3[:, 1, :, :]),
                                            ALU.subtract).then_inc(s_MH, 1)
                    soft.done(nc.vector.tensor_copy(carry[:, :], MH[:, :, MC - 1]))
                    soft.done(nc.vector.tensor_tensor(fz[:, 0, :], m_old[:, :], er_k0, ALU.add))
                    soft.done(nc.vector.tensor_tensor(fz[:, 1, :], MH[:, :, 0], er_k0, ALU.add))
                    soft.after()
                    soft.done(nc.vector.scalar_tensor_tensor(out=fl[:, :, :], in0=fz[:, :, :], scalar=SLOPE, in1=fz[:, :, :],
                                                             op0=ALU.mult, op1=ALU.max))
                    soft.after()
                    nc.vector.tensor_tensor(fd[:, :], fl[:, 0, :], fl[:, 1, :], ALU.subtract).then_inc(s_fd, 1)
                if main:
                    add_in(u - 1, ks)
                if chain:
                    dve.wait_ge(s_mxe, u + 2)
                    dve.wait_ge(s_ers, u + 2)
                    soft.done(nc.vector.tensor_tensor(zz[:, 0, :].rearrange("p (c h) -> p c h", h=H), rows[:, r, :, EX:ROW],
                                                      erS[:, :].rearrange("p (c h) -> p c h", h=H), ALU.add))
                    soft.done(nc.vector.tensor_tensor(zz[:, 1, :], mx_e, erS[:, :], ALU.add))
                    soft.after()
                    soft.done(nc.vector.scalar_tensor_tensor(out=zl[:, :, :], in0=zz[:, :, :], scalar=SLOPE, in1=zz[:, :, :],
                                                             op0=ALU.mult, op1=ALU.max))
                    soft.after()
                    soft.done(nc.vector.tensor_tensor(zl[:, 0, :], zl[:, 0, :], zl[:, 1, :], ALU.subtract))
                    soft.after()
                    nc.vector.tensor_scalar(zd[:, :], zl[:, 0, :], 0.0, None, ALU.min).then_inc(s_zd, 1)
                if chain:
                    masks(u + 1)
                    dve.wait_ge(s_fac, u + 1)
                    if main:
                        dve.wait_ge(s_fl, u * MC + 1)
                    a = acc[:, bass.ds(k0 * RS + HF, D)].rearrange("p (h d) -> p h d", d=DH)
                    soft.done(nc.vector.tensor_tensor(a, a, fac[:, :].unsqueeze(2).to_broadcast([P, H, DH]), ALU.mult))
                    a = acc[:, bass.ds(k0 * RS + EX, H)]
                    soft.done(nc.vector.tensor_tensor(a, a, fac[:, :], ALU.mult))
                    soft.after()
                    dve.wait_ge(s_ex, u + 1)
                    for q in range(Q):
                        cs = slice(q * QC, (q + 1) * QC)
                        a = rows[:, r, cs, HF:EX].rearrange("p c (h d) -> p c h d", d=DH)
                        nc.vector.tensor_tensor(a, a, rows[:, r, cs, EX:ROW].unsqueeze(3).to_broadcast([P, QC, H, DH]),
                                                ALU.mult).then_inc(s_prod, 1)
                    assert soft.n == SOFT, soft.n

            masks(0)
            build(0, 0)
            slot(0, 0, True, False)
            with dve.Fori(0, (NM - 1) // RING) as i:
                for j in range(RING):
                    slot(i * RING + (1 + j), (1 + j) % RING, True, True)
            slot(NM, None, False, True)

            dve.wait_ge(s_fl, COLS + 1)
            EP = 20

            def rows_of(v):
                return v.unsqueeze(2).to_broadcast([P, EB, D])

            def batch(b, loaded):
                ep = Chain(dve, s_ep, b * EP)
                A = acc[:, bass.ds(b * (EB * RS), EB * RS)].rearrange("p (k w) -> p k w", w=RS)
                cnt = A[:, :, ONE:ONE + 1].rearrange("p k o -> p (k o)")
                ep.done(nc.vector.tensor_scalar(den_f, A[:, :, EX:ROW], DEN_FLOOR, None, ALU.max))
                ep.done(nc.vector.tensor_scalar(small(0), cnt, 1.0, None, ALU.max))
                ep.done(nc.vector.tensor_scalar(small(1), cnt, 1.0, None, ALU.add))
                ep.done(nc.vector.tensor_scalar(small(2), cnt, 1.0, None, ALU.min))
                ep.after()
                ep.done(nc.vector.reciprocal(rden_f, den_f))
                ep.done(nc.vector.reciprocal(small(3), small(0)))
                ep.done(nc.vector.reciprocal(small(4), small(1)))
                ep.after()
                nc.vector.tensor_tensor(es_f, A[:, :, 0:D], rows_of(small(3)), ALU.mult).then_inc(s_es, 1)
                ep.done(nc.vector.tensor_tensor(o_f.rearrange("p k (h d) -> p k h d", d=DH),
                                                A[:, :, HF:EX].rearrange("p k (h d) -> p k h d", d=DH),
                                                rden_f.unsqueeze(3).to_broadcast([P, EB, H, DH]), ALU.mult))
                dve.wait_ge(s_lx, loaded)
                ep.done(nc.vector.tensor_tensor(t_f, hf_f, rows_of(small(4)), ALU.mult))
                for other in (t_f, x_f, bias_b[:, :].unsqueeze(1).to_broadcast([P, EB, D])):
                    ep.after()
                    ep.done(nc.vector.tensor_tensor(o_f, o_f, other, ALU.add))
                ep.done(nc.vector.tensor_tensor(t_f, be_b[:, :].unsqueeze(1).to_broadcast([P, EB, D]),
                                                rows_of(small(2)), ALU.mult))
                ep.after()
                ep.done(nc.vector.tensor_tensor(o_f, o_f, t_f, ALU.add))
                dve.wait_ge(s_he, b * EB + EB)
                ep.after()
                for a, tiles in ((0, 4), (1, EB - 4)):
                    v = o_f[:, 4 * a:4 * a + tiles, :]
                    ep.done(nc.vector.tensor_tensor(v, v, ps_main[a][:, 0:tiles * P].rearrange("p (k d) -> p k d", d=D), ALU.add))
                ep.after()
                ep.done(nc.vector.tensor_reduce(small(5), o_f, AX.X, ALU.add))
                ep.after()
                ep.done(nc.vector.tensor_scalar(small(8), small(5), -1.0 / D, None, ALU.mult))
                ep.after()
                nc.vector.tensor_tensor(o_f, o_f, rows_of(small(8)), ALU.add).then_inc(s_sq, 1)
                dve.wait_ge(s_var, b + 1)
                ep.done(nc.vector.tensor_reduce(small(5), t_f, AX.X, ALU.add))
                ep.after()
                nc.vector.tensor_scalar(small(6), small(5), 1.0 / D, LN_EPS, ALU.mult, ALU.add).then_inc(s_std, 1)
                dve.wait_ge(s_rt, b + 1)
                ep.done(nc.vector.reciprocal(small(8), small(7)))
                ep.after()
                dve.wait_ge(s_sq, b + 1)
                nc.vector.tensor_tensor(o_f, o_f, rows_of(small(8)), ALU.mult).then_inc(s_o, 1)
                assert ep.n == EP, ep.n

            with dve.Fori(0, NEB - 1) as b:
                batch(b, b * 32 + 32)
                dve.wait_ge(s_out, b * 16 + 16)
            batch(NEB - 1, (NEB - 1) * 32 + 64)


def kernel(x, src, dst, edge_attr_128, L0_gnn_W_fc, L0_gnn_attn_l, L0_gnn_attn_r, L0_gnn_bias, L0_gnn_W_e, L0_gnn_b_e):
    import concourse.bacc as bacc
    from concourse.bass_utils import run_bass_kernel_spmd

    n, e = x.shape[0], src.shape[0]
    pad = -e % P
    past = -(-n // P) * P - 1
    arrays = {
        "x": x,
        "src": np.pad(np.asarray(src), (0, pad)),
        "dst": np.pad(np.asarray(dst), (0, pad), constant_values=past),
        "edge_attr": np.pad(np.asarray(edge_attr_128), ((0, pad), (0, 0))),
        "w_fc": L0_gnn_W_fc, "attn_l": L0_gnn_attn_l, "attn_r": L0_gnn_attn_r, "bias": L0_gnn_bias,
        "w_e": L0_gnn_W_e, "b_e": L0_gnn_b_e,
    }
    arrays = {k: np.ascontiguousarray(v) for k, v in arrays.items()}
    nc = bacc.Bacc("TRN2", target_bir_lowering=False, num_devices=1)
    args = [nc.dram_tensor(k, v.shape, mybir.dt.from_np(v.dtype), kind="ExternalInput").ap() for k, v in arrays.items()]
    out = nc.dram_tensor("out", x.shape, F32, kind="ExternalOutput").ap()
    gat_layer(nc, *args, out)
    return run_bass_kernel_spmd(nc, [arrays], core_ids=[0]).results[0]["out"]
```

```python
import numpy as np
import concourse.bass as bass
from concourse import mybir
from contextlib import ExitStack

F32 = mybir.dt.float32
I32 = mybir.dt.int32
BF16 = mybir.dt.bfloat16
ENG = mybir.EngineType
ALU = mybir.AluOpType
ACT = mybir.ActivationFunctionType
AX = mybir.AxisListType

P = 128
BIG = float(2.0 ** 100)
BANK = 512
DEN_FLOOR = 1e-30
LN_EPS = 1e-5
SLOPE = 0.2


def top(v):
    return v.bitcast(BF16)[..., 1::2]


class Chain:

    def __init__(self, eng, sem, base):
        self.eng, self.sem, self.base, self.n = eng, sem, base, 0

    def done(self, ins):
        ins.then_inc(self.sem, 1)
        self.n += 1

    def after(self):
        self.eng.wait_ge(self.sem, self.base + self.n)


def gat_layer(nc, x, src, dst, ef, w_fc, attn_l, attn_r, bias, w_e, b_e, out):
    N, D = x.shape
    H, DH = attn_l.shape
    EPAD = src.shape[0]
    ET = EPAD // P
    NT = -(-N // P)
    TAIL = N - (NT - 1) * P
    MC = 16
    COLS = ET + NT + (-(ET + NT)) % MC
    NM = COLS // MC
    NB = -(-COLS // P)
    CP = NB * P
    ACT_BLOCKS = 3
    KD = NT
    RING = 3
    Q = 4
    QC = MC // Q
    ONE, HF, EX, ROW = D, D + 1, 2 * D + 1, 2 * D + 1 + H
    RS = ROW + 1
    TW = D + H
    WC = D + 2 * H
    assert NM == 1 + RING * ((NM - 1) // RING) and MC * H == P
    XC = 4
    NXC = (NT - 1) // XC
    XR = 4
    assert NXC % XR == 0 and NXC * XC == NT - 1
    EB = 7
    NEB = NT // EB
    assert NEB * EB == NT

    with ExitStack() as ctx:
        def sb(name, shape, dt=F32):
            return ctx.enter_context(nc.sbuf_tensor(name, shape, dt))

        def sem(name):
            return ctx.enter_context(nc.semaphore(name))

        ctx.enter_context(nc.allow_non_contiguous_dma(reason="small tables, and one column of dst"))
        node_table = nc.dram_tensor("node_table", (N, TW), F32, kind="Internal").ap()
        tk_dram = nc.dram_tensor("tk_dram", (2, CP), I32, kind="Internal").ap()

        acc = sb("acc", [P, (NT + 1) * RS])
        rows = sb("rows", [P, RING, MC, RS])
        S = sb("S", [P, RING, MC, P])
        Sb = sb("Sb", [P, RING, MC, P], BF16)
        ST = sb("ST", [P, MC, P], BF16)
        er_parts = sb("er_parts", [P, 3, (NT + 1) * H])
        er_tab = er_parts[:, 0, :]
        ident_b = sb("ident_b", [P, P], BF16)
        ident = sb("ident", [P, P])
        iota_row = sb("iota_row", [P, P])
        ones_row = sb("ones_row", [1, P])
        dlocT = sb("dlocT", [P, CP])
        lastT = sb("lastT", [P, CP])
        startT = sb("startT", [P, CP])
        srcT = sb("srcT", [P, CP], I32)
        kmask = sb("kmask", [P, 3, CP])
        ktab = sb("ktab", [1, CP], I32)
        ttab = sb("ttab", [1, CP], I32)
        btab = sb("btab", [1, CP // MC * (MC + 1)], I32)
        zeros_b = sb("zeros_b", [P, P], BF16)
        src_now = sb("src_now", [P, RING, MC], I32)
        start_rep = sb("start_rep", [P, MC, H])
        el_now = sb("el_now", [P, MC, H])
        startS = sb("startS", [P, P])
        runmax = sb("runmax", [P, P])
        V = sb("V", [P, MC, 3, H + 1])
        absent = sb("absent", [P, MC])
        muH = sb("muH", [P, H, MC])
        kf_rep = sb("kf_rep", [P, H, MC])
        kb_rep = sb("kb_rep", [P, H, MC])
        upmax = sb("upmax", [P, P])
        MH = sb("MH", [P, H, MC])
        top_z = sb("top_z", [P, H, MC])
        nodes3 = sb("nodes3", [P, 3, 2 * H, MC])
        L3 = nodes3[:, :, 0:H, :]
        carry = sb("carry", [P, H])
        m_old = sb("m_old", [P, H])
        fz = sb("fz", [P, 2, H])
        fl = sb("fl", [P, 2, H])
        fd = sb("fd", [P, H])
        fac = sb("fac", [P, H])
        zz = sb("zz", [P, P])
        zl = sb("zl", [P, P])
        zd = sb("zd", [P, P])
        w_sb = sb("w_sb", [P, WC])
        we_sb = sb("we_sb", [P, D])
        attn_b = sb("attn_b", [P, 2, D])
        wa = sb("wa", [P, 2, D])
        bias_b = sb("bias_b", [P, D])
        be_b = sb("be_b", [P, D])
        def scratch(first, places, words):
            return (acc[:, first:first + places * XC * words].rearrange("p (h c d) -> p h c d", h=places, c=XC),
                    first + places * XC * words)

        xin, used = scratch(0, XR + 1, D)
        xT, used = scratch(used, 2, P)
        at_stage = used
        stage, used = scratch(used, XR + 1, TW)
        flat = rows[:, :, :, :].rearrange("p a b c -> p (a b c)")
        flat_S = S[:, :, :, :].rearrange("p a b c -> p (a b c)")
        W7 = NB * P

        def piece(n):
            return flat[:, MC * RS + n * W7:MC * RS + (n + 1) * W7]

        def piece_S(n, k=1):
            return flat_S[:, n * W7:(n + k) * W7]

        dcol_i = piece(0).bitcast(I32).rearrange("p (b e) -> p b e", e=P)
        scol_i = piece(1).bitcast(I32).rearrange("p (b e) -> p b e", e=P)
        dcol = piece(2).rearrange("p (b e) -> p b e", e=P)
        scol = piece(3).rearrange("p (b e) -> p b e", e=P)
        dloc = piece(4).rearrange("p (b e) -> p b e", e=P)
        lastc = piece(5).rearrange("p (b e) -> p b e", e=P)
        startc = piece(6).rearrange("p (b e) -> p b e", e=P)
        krow = piece(7)[0:1, :]
        stb = piece_S(0)
        cmp_t = [piece_S(1)] + [piece(n) for n in range(2, NB + 1)]
        first_i = piece_S(2)[0:1, :].bitcast(I32)
        tile_i = piece_S(3)[0:1, :].bitcast(I32)
        first_s = piece_S(4)[0:1, :]
        kmrow = piece_S(0, 3)[0:1, :].rearrange("p (a c) -> p a c", a=3)
        kmrow_b = piece_S(5)[0:1, :]
        sid_i = sb("sid_i", [P, NB], I32)
        sid = sb("sid", [P, NB])
        tcnt = sb("tcnt", [P, NB])
        kcol = sb("kcol", [P, NB])
        k128 = sb("k128", [P, NB])
        t_i = sb("t_i", [P, NB], I32)
        k_i = sb("k_i", [P, NB], I32)

        def bank(name):
            return ctx.enter_context(nc.psum_tensor(name, [P, BANK], F32))

        ps_pair = ctx.enter_context(nc.psum_tensor("ps_pair", [P, 2 * BANK], F32))
        ps_main = [ps_pair[:, 0:BANK], ps_pair[:, BANK:2 * BANK]]
        ps_st = [bank("ps_st0"), bank("ps_st1")]
        ps_x = bank("ps_x")
        ps_f = bank("ps_f")
        ps_e = bank("ps_e")
        ps_t = bank("ps_t")
        ps_proj = [ps_main, [ps_e, ps_t]]
        el_t, start_t = ps_x[:, 0:P], ps_x[:, P:2 * P]
        run_e, mu = ps_f[:, 0:P], ps_f[:, P:P + MC * (H + 1)]
        edge_v = ps_t[:, 0:2 * P].rearrange("p (c w) -> p c w", w=2 * H)
        mx_e, er_e = edge_v[:, :, 0:H], edge_v[:, :, H:2 * H]

        ident_cleared = sem("ident_cleared")
        ident_ready = sem("ident_ready")
        iotas_ready = sem("iotas_ready")
        ones_ready = sem("ones_ready")
        weights_loaded = sem("weights_loaded")
        biases_loaded = sem("biases_loaded")
        firsts_loaded = sem("firsts_loaded")
        weights_joined = sem("weights_joined")
        tail_cleared = sem("tail_cleared")
        x_loaded = [sem(f"x_loaded{n}") for n in range(XR + 1)]
        x_turned = sem("x_turned")
        x_placed = sem("x_placed")
        projection_done = sem("projection_done")
        projection_copied = sem("projection_copied")
        rows_staged = sem("rows_staged")
        table_stored = [sem(f"table_stored{n}") for n in range(XR + 1)]
        pre_steps = sem("pre_steps")
        firsts_summed = sem("firsts_summed")
        firsts_spread = sem("firsts_spread")
        blocks_compared = sem("blocks_compared")
        counts_summed = sem("counts_summed")
        columns_counted = sem("columns_counted")
        src_gathered = sem("src_gathered")
        dst_gathered = sem("dst_gathered")
        tk_stored = sem("tk_stored")
        tk_loaded = sem("tk_loaded")
        columns_ready = sem("columns_ready")
        table_turned = sem("table_turned")
        table_placed = sem("table_placed")
        mask_rows_ready = sem("mask_rows_ready")
        masks_spread = sem("masks_spread")
        masks_placed = sem("masks_placed")
        first_stages_done = sem("first_stages_done")
        indices_placed = sem("indices_placed")
        pool_waited = sem("pool_waited")
        rows_gathered = [sem(f"rows_gathered{n}") for n in range(RING)]
        ef_loaded = [sem(f"ef_loaded{n}") for n in range(RING)]
        onehots_built = sem("onehots_built")
        onehots_widened = sem("onehots_widened")
        onehots_turned = sem("onehots_turned")
        turned_onehots_placed = sem("turned_onehots_placed")
        masks_laid = sem("masks_laid")
        starts_laid = sem("starts_laid")
        el_taken = sem("el_taken")
        el_turned = sem("el_turned")
        starts_placed = sem("starts_placed")
        runs_scanned = sem("runs_scanned")
        runs_turned = sem("runs_turned")
        run_parts_ready = sem("run_parts_ready")
        maxima_at_nodes = sem("maxima_at_nodes")
        er_staged = sem("er_staged")
        node_parts_ready = sem("node_parts_ready")
        node_values_at_edges = sem("node_values_at_edges")
        fac_exponent_ready = sem("fac_exponent_ready")
        fac_ready = sem("fac_ready")
        exponents_ready = sem("exponents_ready")
        edge_weights_ready = sem("edge_weights_ready")
        products_ready = sem("products_ready")
        soft_steps = sem("soft_steps")
        parts_steps = sem("parts_steps")
        columns_summed = sem("columns_summed")
        sums_added = sem("sums_added")
        fin_loaded = [sem(f"fin_loaded{n}") for n in range(2)]
        fin_steps = sem("fin_steps")
        scalars_ready = sem("scalars_ready")
        means_ready = sem("means_ready")
        means_turned = sem("means_turned")
        turned_means_placed = sem("turned_means_placed")
        be_scaled = sem("be_scaled")
        fin_biases_ready = sem("fin_biases_ready")
        edge_part_done = sem("edge_part_done")
        edge_part_added = sem("edge_part_added")
        mean_ready = sem("mean_ready")
        squares_summed = sem("squares_summed")
        variance_ready = sem("variance_ready")
        root_ready = sem("root_ready")
        norm_scalars_ready = sem("norm_scalars_ready")
        out_ready = sem("out_ready")
        out_stored = [sem(f"out_stored{n}") for n in range(2)]
        block = ctx.enter_context(nc.Block())

        def pairs(place):
            a = flat[:, place * MC * RS:place * MC * RS + 4 * EB * D].rearrange("p (n k d) -> p n k d", n=4, d=D)
            return a[:, 0:2, :, :], a[:, 2:4, :, :]

        es_f, esT_f = pairs(0)
        x_f, hf_f = pairs(1)
        t_f, o_f = pairs(2)
        def table_S(n, words):
            return flat_S[:, n * BANK:n * BANK + words]

        den_f = table_S(0, NT * H).rearrange("p (k h) -> p k h", h=H)
        rden_f = table_S(1, NT * H)
        deg_f = table_S(2, NT * 2).rearrange("p (k c) -> p k c", c=2)
        node_f = table_S(3, NT * 3)
        sc_f = table_S(4, 2 * EB * 3).rearrange("p (n k c) -> p n k c", n=2, c=3)
        stat_f = table_S(5, 2 * 7 * EB).rearrange("p (n s k) -> p n s k", n=2, s=7)
        junk_f = flat_S[:, 6 * BANK:6 * BANK + EB * D].rearrange("p (k d) -> p k d", d=D)
        y_f = flat_S[:, 6 * BANK + EB * D:6 * BANK + 3 * EB * D].rearrange("p (n k d) -> p n k d", n=2, d=D)
        SUM, NMEAN, SSQ, VAR, STD, RSTD, NMR = range(7)

        def columns(engine, table, m, n, most, pitch=MC):
            return nc.values_load_multi_w_load_instructions(
                table[0:1, bass.ds(m * pitch, n)], engines=(engine,), min_val=0, max_val=most,
                skip_runtime_bounds_check_because="the tables are counts that end at the shapes' numbers of tiles")[1]

        LOOPS = (NM - 2) // RING
        G16 = MC * 16

        @block.sync
        def _(sp):
            sp.dma_start(w_sb[:, 0:D], w_fc[:, :]).then_inc(weights_loaded, 16)
            sp.dma_start(attn_b[:, 0, :], attn_l.rearrange("h d -> (h d)").partition_broadcast(P)).then_inc(weights_loaded, 16)
            sp.dma_start(attn_b[:, 1, :], attn_r.rearrange("h d -> (h d)").partition_broadcast(P)).then_inc(weights_loaded, 16)
            sp.dma_start(first_i[:, 0:ET], dst.rearrange("(a t e) -> a t e", a=1, e=P)[:, :, 0]).then_inc(firsts_loaded, 16)
            sp.wait_ge(tail_cleared, 1)
            sp.dma_start(xin[0:TAIL, XR, 0, :], x[NXC * XC * P:N, :]).then_inc(x_loaded[XR], 16)
            sp.wait_ge(columns_counted, 1)
            sp.dma_start(tk_dram[0, :].rearrange("(b p) -> p b", p=P), t_i[:, :]).then_inc(tk_stored, 16)
            sp.dma_start(tk_dram[1, :].rearrange("(b p) -> p b", p=P), k_i[:, :]).then_inc(tk_stored, 16)
            sp.wait_ge(tk_stored, 32)
            sp.dma_start(ttab[:, :], tk_dram[0:1, :]).then_inc(tk_loaded, 16)
            sp.dma_start(ktab[:, :], tk_dram[1:2, :]).then_inc(tk_loaded, 16)
            with sp.Fori(0, NXC // XR) as i:
                for h in range(XR):
                    sp.wait_ge(rows_staged, (i * XR + (h + 1)) * 2)
                    sp.dma_start(node_table[bass.ds((i * XR + h) * (XC * P), XC * P), :]
                                 .rearrange("(k p) w -> p k w", p=P), stage[:, h, :, :]).then_inc(table_stored[h], 16)
            sp.wait_ge(rows_staged, NXC * 2 + 1)
            sp.dma_start(node_table[NXC * XC * P:N, :], stage[0:TAIL, XR, 0, :]).then_inc(table_stored[XR], 16)
            sp.dma_start(we_sb[:, :], w_e[:, :]).then_inc(biases_loaded, 16)
            sp.dma_start(bias_b[:, :], bias.partition_broadcast(P)).then_inc(biases_loaded, 16)
            sp.dma_start(be_b[:, :], b_e.partition_broadcast(P)).then_inc(biases_loaded, 16)
            sp.wait_ge(tk_loaded, 32)

            def load_ef(m, r, first):
                ts = columns(ENG.SP, ttab, m, MC, ET - 1)
                for q in range(Q):
                    if not first:
                        sp.wait_ge(columns_summed, (m - RING) * MC + (q + 1) * QC)
                    for c in range(q * QC, (q + 1) * QC):
                        sp.dma_start(rows[:, r, c, 0:D], ef[bass.ds(ts[c] * P, P), :]).then_inc(ef_loaded[r], 16)

            for m in range(RING + 1):
                if m == 1:
                    sp.wait_ge(first_stages_done, 1)
                load_ef(m, m % RING, m < RING)
            with sp.Fori(0, (NM - 1 - RING) // RING) as i:
                for j in range(RING):
                    load_ef(i * RING + (RING + 1 + j), (1 + j) % RING, False)
            def load_fin(b, h, whole):
                for buf, table in ((x_f, x), (hf_f, node_table)):
                    if whole:
                        sp.dma_start(buf[:, h, :, :], table[bass.ds(b * (EB * P), EB * P), 0:D]
                                     .rearrange("(k p) d -> p k d", p=P)).then_inc(fin_loaded[h], 16)
                    else:
                        sp.dma_start(buf[:, h, 0:EB - 1, :], table[b * EB * P:(NT - 1) * P, 0:D]
                                     .rearrange("(k p) d -> p k d", p=P)).then_inc(fin_loaded[h], 16)
                        sp.dma_start(buf[0:TAIL, h, EB - 1, :], table[(NT - 1) * P:N, 0:D]).then_inc(fin_loaded[h], 16)

            def store_fin(b, h):
                sp.wait_ge(out_ready, b + 1)
                sp.dma_start(out[bass.ds(b * (EB * P), EB * P), :].rearrange("(k p) d -> p k d", p=P),
                             y_f[:, h, :, :]).then_inc(out_stored[h], 16)

            def turn_round(b, h, whole):
                sp.wait_ge(edge_part_done, b + 1)
                sp.wait_ge(edge_part_added, b * 2 + 2)
                load_fin(b + 2, h, whole)
                store_fin(b, h)

            sp.wait_ge(columns_summed, (NM - 2) * MC)
            load_fin(0, 0, True)
            load_fin(1, 1, True)
            with sp.Fori(0, (NEB - 3) // 2) as i:
                for h in range(2):
                    turn_round(i * 2 + h, h, True)
            turn_round(NEB - 3, 0, False)
            store_fin(NEB - 2, 1)
            sp.wait_ge(out_ready, NEB)
            sp.dma_start(out[(NEB - 1) * EB * P:(NT - 1) * P, :].rearrange("(k p) d -> p k d", p=P),
                         y_f[:, 0, 0:EB - 1, :]).then_inc(out_stored[0], 16)
            sp.dma_start(out[(NT - 1) * P:N, :], y_f[0:TAIL, 0, EB - 1, :]).then_inc(out_stored[0], 16)
            sp.wait_ge(out_stored[0], (NEB + 1) // 2 * 16 + 32)
            sp.wait_ge(out_stored[1], NEB // 2 * 16 + 16)

        @block.gpsimd
        def _(pool):
            nc.gpsimd.memset(ident[:, :], 0.0).then_inc(ident_cleared, 1)
            pool.wait_ge(ident_cleared, 1)
            nc.gpsimd.affine_select(out=ident[:, :], in_=ident[:, :], compare_op=ALU.not_equal, fill=1.0, base=0,
                                    pattern=[[-1, P]], channel_multiplier=1).then_inc(ident_ready, 1)
            nc.gpsimd.iota(iota_row[:, :], [[1, P]], base=0, channel_multiplier=0,
                           allow_small_or_imprecise_dtypes=True).then_inc(iotas_ready, 1)
            nc.gpsimd.iota(tile_i[:, :], [[1, CP]], base=0, channel_multiplier=0).then_inc(iotas_ready, 1)
            nc.gpsimd.iota(sid_i[:, :], [[P, NB]], base=0, channel_multiplier=1).then_inc(iotas_ready, 1)
            pool.wait_ge(columns_counted, 1)
            for table, into, s in ((src, scol_i, src_gathered), (dst, dcol_i, dst_gathered)):
                for b in range(NB):
                    nc.gpsimd.indirect_dma_start(
                        out=into[:, b, :], out_offset=None, in_=table.rearrange("(t e) -> t e", e=P),
                        in_offset=bass.IndirectOffsetOnAxis(ap=t_i[:, b:b + 1], axis=0)).then_inc(s, 16)
            for h in range(XR):
                pool.wait_ge(table_stored[h], NXC // XR * 16)
            pool.wait_ge(table_stored[XR], 16)

            def gather(m, r, first):
                for q in range(Q):
                    if not first:
                        pool.wait_ge(columns_summed, (m - RING) * MC + (q + 1) * QC)
                        pool.sem_inc(pool_waited, 1)
                    if q == 0:
                        pool.wait_ge(indices_placed, m + 1)
                        pool.sem_inc(pool_waited, 1)
                    for c in range(q * QC, (q + 1) * QC):
                        nc.gpsimd.indirect_dma_start(
                            out=rows[:, r, c, HF:ROW], out_offset=None, in_=node_table[:, :],
                            in_offset=bass.IndirectOffsetOnAxis(ap=src_now[:, r, c:c + 1], axis=0)).then_inc(rows_gathered[r], 16)

            for m in range(RING + 1):
                if m == 1:
                    pool.wait_ge(first_stages_done, 1)
                gather(m, m % RING, m < RING)
            with pool.Fori(0, (NM - 1 - RING) // RING) as i:
                for j in range(RING):
                    gather(i * RING + (RING + 1 + j), (1 + j) % RING, False)

            def biases(b, h, first):
                pool.wait_ge(scalars_ready, b + 1)
                if not first:
                    pool.wait_ge(edge_part_done, b - 1)
                pool.sem_inc(pool_waited, 1)
                if not first:
                    nc.gpsimd.tensor_tensor(es_f[:, h, :, :], acc[:, bass.ds(b * (EB * RS), EB * RS)]
                                            .rearrange("p (k w) -> p k w", w=RS)[:, :, 0:D],
                                            sc_f[:, h, :, 0:1].to_broadcast([P, EB, D]), ALU.mult).then_inc(means_ready, 1)
                nc.gpsimd.tensor_tensor(t_f[:, h, :, :], be_b[:, :].unsqueeze(1).to_broadcast([P, EB, D]),
                                        sc_f[:, h, :, 2:3].to_broadcast([P, EB, D]), ALU.mult).then_inc(be_scaled, 1)
                pool.wait_ge(be_scaled, b + 1)
                pool.sem_inc(pool_waited, 1)
                nc.gpsimd.tensor_tensor(t_f[:, h, :, :], t_f[:, h, :, :], bias_b[:, :].unsqueeze(1)
                                        .to_broadcast([P, EB, D]), ALU.add).then_inc(fin_biases_ready, 1)

            pool.wait_ge(biases_loaded, 48)
            for b in range(2):
                biases(b, b, True)
            with pool.Fori(1, (NEB - 1) // 2) as i:
                for h in range(2):
                    biases(i * 2 + h, h, False)
            biases(NEB - 1, 0, False)

        @block.tensor
        def _(pe):
            pe.wait_ge(ident_ready, 1)
            pe.wait_ge(ones_ready, 1)
            pe.wait_ge(firsts_summed, 1)
            nc.tensor.matmul(ps_x[:, 0:ET // 2], ones_row[:, :], first_s[:, 0:ET // 2], start=True, stop=True)
            nc.tensor.matmul(ps_f[:, 0:ET // 2], ones_row[:, :], first_s[:, ET // 2:2 * (ET // 2)],
                             start=True, stop=True).then_inc(firsts_spread, 1)
            pe.wait_ge(weights_joined, 1)

            def turn_x(c, h, tiles, loaded):
                pe.wait_ge(x_loaded[h], loaded)
                for a in range(tiles):
                    last = nc.tensor.transpose(ps_st[h % 2][:, a * P:(a + 1) * P], xin[:, h, a, :], ident[:, :])
                    last.then_inc(x_turned, 1)

            def project(c, h, tiles):
                pe.wait_ge(x_placed, c + 1)
                for a in range(tiles):
                    if a % 2 == 0:
                        pe.wait_ge(projection_copied, c * 2 + a // 2 + 1)
                    o = ps_proj[h % 2][a // 2][:, (a % 2) * WC:(a % 2) * WC + WC]
                    nc.tensor.matmul(o, xT[:, h % 2, a, :], w_sb[:, 0:WC], start=True, stop=True).then_inc(projection_done, 1)

            turn_x(0, 0, XC, 16)
            with pe.Fori(0, NXC // XR - 1) as i:
                for h in range(XR):
                    turn_x(i * XR + (h + 1), (h + 1) % XR, XC, i * 16 + (1 + (h + 1) // XR) * 16)
                    project(i * XR + h, h, XC)
            for c in range(NXC - XR, NXC):
                if c + 1 < NXC:
                    turn_x(c + 1, (c + 1) % XR, XC, ((c + 1) // XR + 1) * 16)
                else:
                    turn_x(NXC, XR, 1, 16)
                project(c, c % XR, XC)
            project(NXC, XR, 1)
            def turn_table(table, banks):
                for j, bank_ in enumerate(banks):
                    blocks = range(j * 4, min(NB, j * 4 + 4))
                    for b in blocks:
                        last = nc.tensor.transpose(bank_[:, (b % 4) * P:(b % 4 + 1) * P], table[:, b, :], ident[:, :])
                    last.then_inc(table_turned, 1)

            pe.wait_ge(columns_ready, 1)
            pe.wait_ge(projection_copied, NXC * 2 + 5)
            turn_table(scol, (ps_e, ps_t))
            pe.wait_ge(columns_ready, 2)
            turn_table(dloc, (ps_x, ps_f))
            turn_table(lastc, ps_st)
            pe.wait_ge(table_placed, 2)
            turn_table(startc, (ps_e, ps_t))
            pe.wait_ge(mask_rows_ready, 1)
            pe.wait_ge(projection_copied, NXC * 2 + 5)
            half = CP // 2
            for a in range(3):
                for j in range(2):
                    n = a * 2 + j
                    if n >= 2:
                        pe.wait_ge(masks_placed, n - 1)
                    nc.tensor.matmul(ps_main[n % 2][:, 0:half], ones_row[:, :], kmrow[:, a, j * half:(j + 1) * half],
                                     start=True, stop=True).then_inc(masks_spread, 1)
            pe.wait_ge(first_stages_done, 1)

            def exact(o, one_hot, parts):
                for s, part in enumerate(parts):
                    last = nc.tensor.matmul(o, one_hot, part, start=s == 0, stop=s == 2)
                return last

            def sums(m, r, round_m):
                banks = columns(ENG.PE, btab, m, MC + 1, 1, MC + 1)
                pe.wait_ge(ef_loaded[r], round_m)
                pe.wait_ge(onehots_widened, m + 1)
                pe.wait_ge(sums_added, m * MC + 1)
                with pe.If(banks[MC] < 1):
                    for c in range(MC):
                        if c % QC == 0:
                            pe.wait_ge(products_ready, m * Q + c // QC + 1)
                        if c == 0:
                            nc.tensor.matmul(ps_main[1][:, 0:ROW], zeros_b[:, :], Sb[:, r, 0:3, :]
                                             .rearrange("p c n -> p (c n)")[:, 0:ROW], start=True, stop=False,
                                             skip_group_check=True)
                            o = ps_main[0][:, 0:ROW]
                        else:
                            o = ps_pair[:, bass.ds(banks[c] * BANK, ROW)]
                        nc.tensor.matmul(o, S[:, r, c, :], rows[:, r, c, 0:ROW], start=c == 0, stop=True,
                                         skip_group_check=True).then_inc(columns_summed, 1)
                with pe.Else():
                    for c in range(MC):
                        if c % QC == 0:
                            pe.wait_ge(products_ready, m * Q + c // QC + 1)
                        if c > 0:
                            pe.wait_ge(sums_added, m * MC + (c + 1))
                        nc.tensor.matmul(ps_main[0][:, 0:ROW], S[:, r, c, :], rows[:, r, c, 0:ROW],
                                         start=True, stop=True, skip_group_check=True).then_inc(columns_summed, 1)

            def turn_el(m):
                pe.wait_ge(starts_laid, m + 1)
                nc.tensor.transpose(start_t, start_rep[:, :, :].rearrange("p c h -> p (c h)"), ident[:, :])
                pe.wait_ge(el_taken, m + 1)
                nc.tensor.transpose(el_t, el_now[:, :, :].rearrange("p c h -> p (c h)"), ident[:, :]).then_inc(el_turned, 1)

            def turn_runs(m):
                pe.wait_ge(runs_scanned, m + 1)
                nc.tensor.transpose(run_e, runmax[:, :], ident[:, :]).then_inc(runs_turned, 1)

            def turn_S(m, r):
                pe.wait_ge(onehots_built, m + 1)
                for h in range(2):
                    pe.wait_ge(turned_onehots_placed, m * 2 + h + 1)
                    for a in range(MC // 2):
                        last = nc.tensor.transpose(ps_st[h][:, :].bitcast(BF16)[:, a * P:(a + 1) * P],
                                                   Sb[:, r, h * (MC // 2) + a, :], ident_b[:, :])
                    last.then_inc(onehots_turned, 1)

            def maxima_to_nodes(m, r):
                pe.wait_ge(run_parts_ready, m + 1)
                for c in range(MC):
                    last = exact(mu[:, c * (H + 1):(c + 1) * (H + 1)], Sb[:, r, c, :],
                                 [top(V[:, c, s, :]) for s in range(3)])
                last.then_inc(maxima_at_nodes, 1)

            def to_edges(m):
                pe.wait_ge(turned_onehots_placed, m * 2 + 4)
                pe.wait_ge(er_staged, m * MC + MC)
                pe.wait_ge(node_parts_ready, m + 1)
                for c in range(MC):
                    last = exact(edge_v[:, c, :], ST[:, c, :], [top(nodes3[:, s, :, :])[:, :, c] for s in range(3)])
                last.then_inc(node_values_at_edges, 1)

            def slot(u, rn, rm, round_m, begin):
                if not begin:
                    to_edges(u)
                if rm is not None:
                    sums(u - 1, rm, round_m)
                if begin:
                    turn_el(u + 1)
                    to_edges(u)
                if begin:
                    turn_runs(u + 1)
                    turn_S(u + 1, rn)
                    maxima_to_nodes(u + 1, rn)

            turn_el(0)
            turn_S(0, 0)
            turn_runs(0)
            maxima_to_nodes(0, 0)
            slot(0, 1, None, None, True)
            with pe.Fori(0, LOOPS) as i:
                for j in range(RING):
                    slot(i * RING + (1 + j), (2 + j) % RING, j, i * G16 + G16, True)
            for u in range(LOOPS * RING + 1, NM):
                slot(u, (u + 1) % RING, (u - 1) % RING, ((u - 1) // RING + 1) * G16, u + 1 < NM)
            sums(NM - 1, (NM - 1) % RING, ((NM - 1) // RING + 1) * G16)

            pe.wait_ge(biases_loaded, 48)

            def edge_part(b, h, loaded, first):
                pe.wait_ge(means_ready, b + 1)
                for k in range(EB):
                    last = nc.tensor.transpose(ps_st[k // 4][:, (k % 4) * P:(k % 4 + 1) * P], es_f[:, h, k, :], ident[:, :])
                    if k % 4 == 3 or k == EB - 1:
                        last.then_inc(means_turned, 1)
                pe.wait_ge(fin_loaded[h], loaded)
                if not first:
                    pe.wait_ge(edge_part_added, b * 2 - 2)

                def part(k):
                    return ps_proj[h][k // 4][:, (k % 4) * P:(k % 4 + 1) * P]

                for k in range(EB):
                    nc.tensor.matmul(part(k), ident[:, :], x_f[:, h, k, :], start=k % 4 == 0, stop=False,
                                     skip_group_check=True)
                pe.wait_ge(fin_biases_ready, b + 1)
                for k in range(EB):
                    nc.tensor.matmul(part(k), ident[:, :], t_f[:, h, k, :], start=False, stop=False, skip_group_check=True)
                pe.wait_ge(turned_means_placed, b * 2 + 2)
                for k in range(EB):
                    last = nc.tensor.matmul(part(k), esT_f[:, h, k, :], we_sb[:, :], start=False, stop=True,
                                            skip_group_check=True)
                last.then_inc(edge_part_done, 1)

            for b in range(2):
                edge_part(b, b, 32, True)
            with pe.Fori(1, (NEB - 1) // 2) as i:
                for h in range(2):
                    edge_part(i * 2 + h, h, i * 32 + 32, False)
            edge_part(NEB - 1, 0, NEB // 2 * 32 + 64, False)

        @block.scalar
        def _(act):
            def load_x(c, h):
                act.dma_start(xin[:, h, :, :],
                              x[bass.ds(c * (XC * P), XC * P), :].rearrange("(k p) d -> p k d", p=P)).then_inc(x_loaded[h], 16)

            def turned(c, h, tiles):
                act.wait_ge(x_turned, c * XC + tiles)
                nc.scalar.activation(xT[:, h % 2, 0:tiles, :].rearrange("p k d -> p (k d)"),
                                     ps_st[h % 2][:, 0:tiles * P], ACT.Copy).then_inc(x_placed, 1)

            def results(c, h, tiles, stored=None):
                for g in range(-(-tiles // 2)):
                    k = min(2, tiles - 2 * g)
                    if g == 0 and stored is not None:
                        act.wait_ge(table_stored[h], stored)
                    act.wait_ge(projection_done, c * XC + 2 * g + k)
                    v = ps_proj[h % 2][g][:, 0:k * WC].rearrange("p (k w) -> p k w", w=WC)
                    nc.scalar.activation(stage[:, h, 2 * g:2 * g + k, :], v[:, :, 0:TW], ACT.Copy).then_inc(rows_staged, 1)
                    nc.scalar.activation(er_tab[:, bass.ds((c * XC + 2 * g) * H, k * H)]
                                         .rearrange("p (k h) -> p k h", h=H), v[:, :, TW:WC], ACT.Copy).then_inc(projection_copied, 1)

            act.sem_inc(projection_copied, 4)
            for h in range(XR):
                load_x(h, h)
            for b in range(NB - ACT_BLOCKS, NB):
                act.wait_ge(blocks_compared, b - (NB - ACT_BLOCKS) + 1)
                nc.scalar.activation(cmp_t[b][:, 1:ET], cmp_t[b][:, 1:ET], ACT.Copy,
                                     accum_out=tcnt[:, b:b + 1]).then_inc(counts_summed, 1)
            turned(0, 0, XC)
            for c in range(XR):
                turned(c + 1, (c + 1) % XR, XC)
                load_x(c + XR, c)
                results(c, c, XC)
            with act.Fori(1, NXC // XR - 1) as i:
                for h in range(XR):
                    turned(i * XR + (h + 1), (h + 1) % XR, XC)
                    load_x(i * XR + (h + XR), h)
                    results(i * XR + h, h, XC, i * 16)
            for c in range(NXC - XR, NXC):
                if c + 1 < NXC:
                    turned(c + 1, (c + 1) % XR, XC)
                else:
                    turned(NXC, XR, 1)
                results(c, c % XR, XC, c // XR * 16)
            results(NXC, XR, 1)

            def place_tables(n, table, banks):
                for j, bank_ in enumerate(banks):
                    w = min(CP, (j + 1) * BANK) - j * BANK
                    act.wait_ge(table_turned, n + j + 1)
                    nc.scalar.activation(table[:, j * BANK:j * BANK + w], bank_[:, 0:w], ACT.Copy).then_inc(table_placed, 1)

            place_tables(0, srcT, (ps_e, ps_t))
            act.wait_ge(table_placed, 2)

            def indices(m, r):
                nc.scalar.activation(src_now[:, r, :], srcT[:, bass.ds(m * MC, MC)], ACT.Copy).then_inc(indices_placed, 1)

            for m in range(RING):
                indices(m, m)
            place_tables(2, dlocT, (ps_x, ps_f))
            place_tables(4, lastT, ps_st)
            place_tables(6, startT, (ps_e, ps_t))
            half = CP // 2
            for a in range(3):
                for j in range(2):
                    n = a * 2 + j
                    act.wait_ge(masks_spread, n + 1)
                    nc.scalar.activation(kmask[:, a, j * half:(j + 1) * half], ps_main[n % 2][:, 0:half],
                                         ACT.Copy).then_inc(masks_placed, 1)

            act.wait_ge(first_stages_done, 1)
            act.sem_inc(turned_onehots_placed, 2)

            def place_ST(m, h):
                if h == 0:
                    act.wait_ge(node_values_at_edges, m + 1)
                act.wait_ge(onehots_turned, m * 2 + h + 1)
                nc.scalar.activation(ST[:, h * (MC // 2):(h + 1) * (MC // 2), :].rearrange("p c n -> p (c n)"),
                                     ps_st[h][:, :].bitcast(BF16), ACT.Copy).then_inc(turned_onehots_placed, 1)

            def stage_er(m):
                ks = columns(ENG.Activation, ktab, m, MC, KD)
                for c in range(MC):
                    nc.scalar.activation(nodes3[:, :, H:2 * H, c], er_parts[:, :, bass.ds(ks[c] * H, H)], ACT.Copy).then_inc(er_staged, 1)

            def take_el(m, r, round_g):
                act.wait_ge(rows_gathered[r], round_g)
                nc.scalar.activation(el_now[:, :, :], rows[:, r, :, EX:ROW], ACT.Copy).then_inc(el_taken, 1)
                act.wait_ge(el_turned, m + 1)
                nc.scalar.activation(startS[:, :], start_t, ACT.Copy).then_inc(starts_placed, 1)
                indices(m + RING, r)

            def weights(m, r):
                act.wait_ge(exponents_ready, m + 1)
                nc.scalar.activation(rows[:, r, :, EX:ROW], zd[:, :].rearrange("p (c h) -> p c h", h=H),
                                     ACT.Exp).then_inc(edge_weights_ready, 1)

            def widen(m, r):
                act.wait_ge(onehots_built, m + 1)
                nc.scalar.activation(S[:, r, :, :], Sb[:, r, :, :], ACT.Copy).then_inc(onehots_widened, 1)

            def slot(u, r, rn, round_n, begin):
                stage_er(u)
                act.wait_ge(fac_exponent_ready, u + 1)
                nc.scalar.activation(fac[:, :], fd[:, :], ACT.Exp).then_inc(fac_ready, 1)
                if begin:
                    take_el(u + 1, rn, round_n)
                    place_ST(u + 1, 0)
                weights(u, r)
                if begin:
                    place_ST(u + 1, 1)
                    widen(u + 1, rn)

            act.sem_inc(node_values_at_edges, 1)
            take_el(0, 0, G16)
            place_ST(0, 0)
            place_ST(0, 1)
            widen(0, 0)
            slot(0, 0, 1, G16, True)
            with act.Fori(0, LOOPS) as i:
                for j in range(RING):
                    slot(i * RING + (1 + j), (1 + j) % RING, (2 + j) % RING,
                         i * G16 + (1 + (2 + j) // RING) * G16, True)
            for u in range(LOOPS * RING + 1, NM):
                slot(u, u % RING, (u + 1) % RING, ((u + 1) // RING + 1) * G16, u + 1 < NM)

            def turned_edges(b, h):
                for a, tiles in ((0, 4), (1, EB - 4)):
                    act.wait_ge(means_turned, b * 2 + (a + 1))
                    nc.scalar.activation(esT_f[:, h, 4 * a:4 * a + tiles, :].rearrange("p k d -> p (k d)"),
                                         ps_st[a][:, 0:tiles * P], ACT.Copy).then_inc(turned_means_placed, 1)

            def norm(b, h, more, stored):
                if more:
                    turned_edges(b + 1, 1 - h)
                act.wait_ge(mean_ready, b + 1)
                for k in range(EB):
                    last = nc.scalar.activation(junk_f[:, k, :], o_f[:, h, k, :], ACT.Square,
                                                bias=stat_f[:, h, NMEAN, k:k + 1], accum_out=stat_f[:, h, SSQ, k:k + 1])
                last.then_inc(squares_summed, 1)
                act.wait_ge(variance_ready, b + 1)
                nc.scalar.activation(stat_f[:, h, STD, :], stat_f[:, h, VAR, :], ACT.Sqrt).then_inc(root_ready, 1)
                act.wait_ge(norm_scalars_ready, b + 1)
                act.wait_ge(out_stored[h], stored)
                for k in range(EB):
                    last = nc.scalar.activation(y_f[:, h, k, :], o_f[:, h, k, :], ACT.Identity,
                                                bias=stat_f[:, h, NMR, k:k + 1], scale=stat_f[:, h, RSTD, k:k + 1])
                last.then_inc(out_ready, 1)

            def root_tables(n):
                nc.scalar.activation(fz[0:1, 0, n:n + 1], ident[0:1, 0:1], ACT.Sqrt)

            for h in range(2):
                act.sem_inc(out_stored[h], 16)
            root_tables(0)
            turned_edges(0, 0)
            with act.Fori(0, (NEB - 1) // 2) as i:
                root_tables(1)
                for h in range(2):
                    norm(i * 2 + h, h, True, i * 16 + 16)
            norm(NEB - 1, 0, False, NEB // 2 * 16 + 16)

        @block.vector
        def _(dve):
            pre = Chain(dve, pre_steps, 0)
            nc.vector.memset(ones_row[:, :], 1.0).then_inc(ones_ready, 1)
            nc.vector.memset(xin[:, XR, 0, :], 0.0).then_inc(tail_cleared, 1)
            dve.wait_ge(weights_loaded, 48)
            for a in range(2):
                pre.done(nc.vector.tensor_tensor(wa[:, a, :], w_sb[:, 0:D], attn_b[:, a, :], ALU.mult))
            pre.after()
            nc.vector.tensor_reduce(w_sb[:, D:WC].rearrange("p (a h) -> p a h", h=H),
                                    wa[:, :, :].rearrange("p a (h d) -> p a h d", d=DH),
                                    AX.X, ALU.add).then_inc(weights_joined, 1)
            dve.wait_ge(firsts_loaded, 16)
            dve.wait_ge(iotas_ready, 3)
            pre.done(nc.vector.tensor_single_scalar(first_i[:, 0:ET], first_i[:, 0:ET], P.bit_length() - 1,
                                                    ALU.arith_shift_right))
            pre.after()
            nc.vector.tensor_tensor(first_s[:, 0:ET], first_i[:, 0:ET], tile_i[:, 0:ET], ALU.add).then_inc(firsts_summed, 1)
            pre.done(nc.vector.tensor_copy(sid[:, :], sid_i[:, :]))

            dve.wait_ge(firsts_spread, 1)
            for j, p_ in enumerate((ps_x, ps_f)):
                pre.done(nc.vector.tensor_copy(stb[:, j * (ET // 2):(j + 1) * (ET // 2)], p_[:, 0:ET // 2]))
            pre.after()
            def at_or_before(b):
                return nc.vector.tensor_scalar(cmp_t[b][:, 1:ET], stb[:, 1:ET], sid[:, b:b + 1], None, ALU.is_le)

            for b in range(NB - ACT_BLOCKS, NB):
                at_or_before(b).then_inc(blocks_compared, 1)
            for b in range(NB - ACT_BLOCKS):
                pre.done(at_or_before(b))
            pre.after()
            for b in range(NB - ACT_BLOCKS):
                pre.done(nc.vector.tensor_reduce(tcnt[:, b:b + 1], cmp_t[b][:, 1:ET], AX.X, ALU.add))
            dve.wait_ge(counts_summed, ACT_BLOCKS)
            pre.after()
            pre.done(nc.vector.tensor_tensor(kcol[:, :], sid[:, :], tcnt[:, :], ALU.subtract))
            pre.after()
            pre.done(nc.vector.tensor_scalar(kcol[:, :], kcol[:, :], float(KD), None, ALU.min))
            pre.done(nc.vector.tensor_copy(t_i[:, :], tcnt[:, :]))
            pre.after()
            pre.done(nc.vector.tensor_scalar(k128[:, :], kcol[:, :], float(P), None, ALU.mult))
            pre.done(nc.vector.tensor_copy(k_i[:, :], kcol[:, :]))
            pre.after()
            dve.sem_inc(columns_counted, 1)

            pre.done(nc.vector.memset(er_tab[:, NT * H:(NT + 1) * H], 0.0))
            dve.wait_ge(ident_ready, 1)
            pre.done(nc.vector.tensor_copy(ident_b[:, :], ident[:, :]))
            pre.done(nc.vector.memset(zeros_b[:, :], 0.0))

            dve.wait_ge(tk_loaded, 32)
            pre.done(nc.vector.tensor_copy(krow, ktab[:, :]))
            pre.after()
            pre.done(nc.vector.tensor_tensor(kmrow[:, 0, 1:CP], krow[:, 1:CP], krow[:, 0:CP - 1], ALU.not_equal))
            pre.done(nc.vector.memset(kmrow[:, 0, 0:1], 1.0))
            pre.after()
            pre.done(nc.vector.tensor_scalar(kmrow[:, 1, :], kmrow[:, 0, :], -BIG, None, ALU.mult))
            pre.done(nc.vector.tensor_scalar(kmrow[:, 2, 0:CP - 1], kmrow[:, 0, 1:CP], -BIG, None, ALU.mult))
            pre.after()
            pre.done(nc.vector.tensor_copy(kmrow[:, 0, :], kmrow[:, 1, :]))
            pre.after()
            by_macro = kmrow.rearrange("p a (m c) -> p a m c", c=MC)
            pre.done(nc.vector.memset(by_macro[:, 1, :, 0:1], -BIG))
            pre.done(nc.vector.memset(by_macro[:, 2, :, MC - 1:MC], -BIG))
            pre.after()
            dve.sem_inc(mask_rows_ready, 1)
            k_mac = krow.rearrange("p (m c) -> p m c", c=MC)
            b_mac = kmrow_b.rearrange("p (m c) -> p m c", c=MC)
            k_first = k_mac[:, :, 0:1].to_broadcast([1, CP // MC, MC])
            pre.done(nc.vector.tensor_tensor(b_mac, k_mac, k_first, ALU.subtract))
            pre.after()
            by_macro = btab[:, :].rearrange("p (m c) -> p m c", c=MC + 1)
            pre.done(nc.vector.tensor_scalar(by_macro[:, :, 0:MC], b_mac, 1.0, None, ALU.min))
            pre.after()
            pre.done(nc.vector.tensor_scalar(b_mac[:, :, MC - 1:MC], b_mac[:, :, MC - 1:MC], -1.0, 0.0, ALU.add, ALU.max))
            pre.after()
            pre.done(nc.vector.tensor_scalar(by_macro[:, :, MC:MC + 1], b_mac[:, :, MC - 1:MC], 1.0, None, ALU.min))

            dve.wait_ge(src_gathered, NB * 16)
            nc.vector.tensor_copy(scol, scol_i).then_inc(columns_ready, 1)

            pre.after()
            dve.wait_ge(dst_gathered, NB * 16)
            pre.done(nc.vector.tensor_copy(dcol, dcol_i))
            pre.after()
            pre.done(nc.vector.tensor_tensor(dloc, dcol, k128[:, :].unsqueeze(2).to_broadcast([P, NB, P]), ALU.subtract))
            pre.done(nc.vector.tensor_tensor(lastc[:, :, 0:P - 1], dcol[:, :, 0:P - 1], dcol[:, :, 1:P], ALU.not_equal))
            pre.done(nc.vector.memset(lastc[:, :, P - 1:P], 1.0))
            pre.after()
            pre.done(nc.vector.tensor_scalar(startc[:, :, 1:P], lastc[:, :, 0:P - 1], -BIG, None, ALU.mult))
            pre.done(nc.vector.memset(startc[:, :, 0:1], -BIG))
            pre.after()
            dve.sem_inc(columns_ready, 1)

            dve.wait_ge(projection_copied, NXC * 2 + 5)
            pre.done(nc.vector.tensor_tensor(er_parts[:, 1, :], er_parts[:, 0, :], top(er_parts[:, 0, :]), ALU.subtract))
            pre.after()
            pre.done(nc.vector.tensor_tensor(er_parts[:, 2, :], er_parts[:, 1, :], top(er_parts[:, 1, :]), ALU.subtract))

            pre.done(nc.vector.memset(acc[:, used:], 0.0))
            pre.done(nc.vector.memset(acc[:, 0:at_stage], 0.0))

            dve.wait_ge(table_placed, 8)
            pre.after()
            dve.wait_ge(masks_placed, 6)
            pre.done(nc.vector.memset(rows[:, :, :, ONE:ONE + 1], 1.0))
            pre.done(nc.vector.memset(carry[:, :], -BIG))
            pre.after()
            dve.sem_inc(first_stages_done, 1)
            dve.sem_inc(sums_added, 1)

            def masks(m):
                cols = bass.ds(m * MC, MC)
                for rep_, table in ((kf_rep, kmask[:, 1, cols]), (kb_rep, kmask[:, 2, cols])):
                    nc.vector.tensor_scalar(rep_[:, :, :], table.unsqueeze(1).to_broadcast([P, H, MC]), 1.0, None,
                                            ALU.mult).then_inc(masks_laid, 1)

            def starts(m):
                nc.vector.tensor_scalar(start_rep[:, :, :], startT[:, bass.ds(m * MC, MC)].unsqueeze(2)
                                        .to_broadcast([P, MC, H]), 1.0, None, ALU.mult).then_inc(starts_laid, 1)

            def build(m, r):
                cols = bass.ds(m * MC, MC)
                nc.vector.tensor_tensor(Sb[:, r, :, :], iota_row[:, :].unsqueeze(1).to_broadcast([P, MC, P]),
                                        dlocT[:, cols].unsqueeze(2).to_broadcast([P, MC, P]),
                                        ALU.is_equal).then_inc(onehots_built, 1)

            def add_in(m, ks):
                def add(k, bank_):
                    a = acc[:, bass.ds(k * RS, ROW)]
                    return nc.vector.tensor_tensor(a, a, ps_main[bank_][:, 0:ROW], ALU.add)

                with dve.If(ks[MC - 1] - ks[0] < 2):
                    dve.wait_ge(columns_summed, m * MC + MC)
                    add(ks[0], 0).then_inc(sums_added, MC // 2)
                    dve.wait_ge(sums_added, m * MC + (MC // 2 + 1))
                    add(ks[MC - 1], 1).then_inc(sums_added, MC // 2)
                with dve.Else():
                    for c in range(MC):
                        dve.wait_ge(columns_summed, m * MC + (c + 1))
                        dve.wait_ge(sums_added, m * MC + (c + 1))
                        add(ks[c], 0).then_inc(sums_added, 1)

            def run_maxima(m):
                dve.wait_ge(starts_placed, m + 1)
                nc.vector.tensor_tensor_scan(runmax[:, :], startS[:, :], el_t, -BIG, ALU.add, ALU.max).then_inc(runs_scanned, 1)

            PARTS = 3
            SOFT = 18

            def speakers(m, parts):
                last = lastT[:, bass.ds(m * MC, MC)].unsqueeze(2)
                dve.wait_ge(runs_turned, m + 1)
                parts.done(nc.vector.tensor_tensor(V[:, :, 0, 0:H], run_e.rearrange("p (c h) -> p c h", h=H),
                                                   last.to_broadcast([P, MC, H]), ALU.mult))
                parts.done(nc.vector.tensor_scalar(V[:, :, 0, H:H + 1], last, 1.0, None, ALU.mult))

            def second_part(parts):
                parts.after()
                parts.done(nc.vector.tensor_tensor(V[:, :, 1, :], V[:, :, 0, :], top(V[:, :, 0, :]), ALU.subtract))

            def third_part(parts):
                parts.after()
                nc.vector.tensor_tensor(V[:, :, 2, :], V[:, :, 1, :], top(V[:, :, 1, :]), ALU.subtract).then_inc(run_parts_ready, 1)
                assert parts.n == PARTS, parts.n

            def slot(u, r, rnn, main, begin, ahead):
                if main:
                    ks = columns(ENG.DVE, ktab, u - 1, MC + 1, KD)
                else:
                    ks = columns(ENG.DVE, ktab, u, 1, KD)
                k0 = ks[-1]
                soft = Chain(dve, soft_steps, u * SOFT)
                er_k0 = er_tab[:, bass.ds(k0 * H, H)]
                mu_v = mu.rearrange("p (c w) -> p c w", w=H + 1)
                dve.wait_ge(maxima_at_nodes, u + 1)
                soft.done(nc.vector.tensor_scalar(absent[:, :], mu_v[:, :, H:H + 1].rearrange("p c o -> p (c o)"),
                                                  BIG, -BIG, ALU.mult, ALU.add))
                soft.done(nc.vector.tensor_tensor(m_old[:, :], carry[:, :],
                                                  kmask[:, 0, bass.ds(u * MC, 1)].to_broadcast([P, H]), ALU.add))
                soft.after()
                soft.done(nc.vector.tensor_tensor(muH[:, :, :].rearrange("p h c -> p c h"), mu_v[:, :, 0:H],
                                                  absent[:, :].unsqueeze(2).to_broadcast([P, MC, H]), ALU.add))
                soft.after()
                soft.done(nc.vector.tensor_tensor(muH[:, :, 0], muH[:, :, 0], m_old[:, :], ALU.max))
                dve.wait_ge(masks_laid, u * 2 + 2)
                soft.after()
                soft.done(nc.vector.tensor_tensor_scan(upmax[:, :], kf_rep[:, :, :].rearrange("p h c -> p (h c)"),
                                                       muH[:, :, :].rearrange("p h c -> p (h c)"), -BIG,
                                                       ALU.add, ALU.max))
                soft.after()
                soft.done(nc.vector.tensor_tensor_scan(MH.rearrange("p h c -> p (h c)")[:, ::-1],
                                                       kb_rep[:, :, :].rearrange("p h c -> p (h c)")[:, ::-1],
                                                       upmax[:, ::-1], -BIG, ALU.add, ALU.max))
                soft.after()
                dve.wait_ge(er_staged, u * MC + MC)
                soft.done(nc.vector.tensor_tensor(top_z[:, :, :], MH[:, :, :], nodes3[:, 0, H:2 * H, :], ALU.add))
                soft.after()
                soft.done(nc.vector.scalar_tensor_tensor(out=L3[:, 0, :, :], in0=top_z[:, :, :], scalar=SLOPE,
                                                         in1=top_z[:, :, :], op0=ALU.mult, op1=ALU.max))
                soft.after()
                soft.done(nc.vector.tensor_tensor(L3[:, 1, :, :], L3[:, 0, :, :], top(L3[:, 0, :, :]), ALU.subtract))
                soft.after()
                nc.vector.tensor_tensor(L3[:, 2, :, :], L3[:, 1, :, :], top(L3[:, 1, :, :]),
                                        ALU.subtract).then_inc(node_parts_ready, 1)
                soft.done(nc.vector.tensor_copy(carry[:, :], MH[:, :, MC - 1]))
                soft.done(nc.vector.tensor_tensor(fz[:, 0, :], m_old[:, :], er_k0, ALU.add))
                soft.done(nc.vector.tensor_tensor(fz[:, 1, :], MH[:, :, 0], er_k0, ALU.add))
                soft.after()
                soft.done(nc.vector.scalar_tensor_tensor(out=fl[:, :, :], in0=fz[:, :, :], scalar=SLOPE, in1=fz[:, :, :],
                                                         op0=ALU.mult, op1=ALU.max))
                soft.after()
                nc.vector.tensor_tensor(fd[:, :], fl[:, 0, :], fl[:, 1, :], ALU.subtract).then_inc(fac_exponent_ready, 1)
                if main and begin:
                    add_in(u - 1, ks)
                if begin:
                    run_maxima(u + 1)
                parts = Chain(dve, parts_steps, (u + 1) * PARTS)
                dve.wait_ge(node_values_at_edges, u + 2)
                soft.done(nc.vector.tensor_tensor(zz[:, :].rearrange("p (c h) -> p c h", h=H), rows[:, r, :, EX:ROW],
                                                  er_e, ALU.add))
                if begin:
                    speakers(u + 1, parts)
                soft.after()
                soft.done(nc.vector.scalar_tensor_tensor(out=zl[:, :], in0=zz[:, :], scalar=SLOPE, in1=zz[:, :],
                                                         op0=ALU.mult, op1=ALU.max))
                if begin:
                    second_part(parts)
                soft.after()
                zl_c = zl[:, :].rearrange("p (c h) -> p c h", h=H)
                soft.done(nc.vector.tensor_tensor(zl_c, zl_c, mx_e, ALU.subtract))
                if begin:
                    third_part(parts)
                soft.after()
                nc.vector.tensor_scalar(zd[:, :], zl[:, :], 0.0, None, ALU.min).then_inc(exponents_ready, 1)

                def rescale():
                    dve.wait_ge(fac_ready, u + 1)
                    if main:
                        dve.wait_ge(sums_added, u * MC + 1)
                    a = acc[:, bass.ds(k0 * RS + HF, D)].rearrange("p (h d) -> p h d", d=DH)
                    soft.done(nc.vector.tensor_tensor(a, a, fac[:, :].unsqueeze(2).to_broadcast([P, H, DH]), ALU.mult))
                    a = acc[:, bass.ds(k0 * RS + EX, H)]
                    soft.done(nc.vector.tensor_tensor(a, a, fac[:, :], ALU.mult))
                    soft.after()

                if begin:
                    rescale()
                dve.wait_ge(edge_weights_ready, u + 1)
                for q in range(Q):
                    cs = slice(q * QC, (q + 1) * QC)
                    a = rows[:, r, cs, HF:EX].rearrange("p c (h d) -> p c h d", d=DH)
                    nc.vector.tensor_tensor(a, a, rows[:, r, cs, EX:ROW].unsqueeze(3).to_broadcast([P, QC, H, DH]),
                                            ALU.mult).then_inc(products_ready, 1)
                if not begin:
                    add_in(u - 1, ks)
                    rescale()
                assert soft.n == SOFT, soft.n
                if begin:
                    masks(u + 1)
                if ahead:
                    build(u + 2, rnn)
                    starts(u + 2)

            masks(0)
            starts(0)
            build(0, 0)
            for h in range(XR):
                dve.wait_ge(table_stored[h], NXC // XR * 16)
            dve.wait_ge(table_stored[XR], 16)
            pre.done(nc.vector.memset(acc[:, at_stage:used], 0.0))
            pre.after()
            run_maxima(0)
            parts = Chain(dve, parts_steps, 0)
            speakers(0, parts)
            second_part(parts)
            third_part(parts)
            build(1, 1)
            starts(1)
            slot(0, 0, 2, False, True, True)
            with dve.Fori(0, LOOPS) as i:
                for j in range(RING):
                    slot(i * RING + (1 + j), (1 + j) % RING, j % RING, True, True, True)
            for u in range(LOOPS * RING + 1, NM):
                slot(u, u % RING, (u + 2) % RING, True, u + 1 < NM, u + 2 < NM)
            add_in(NM - 1, columns(ENG.DVE, ktab, NM - 1, MC, KD))

            dve.wait_ge(sums_added, COLS + 1)
            FIRST, EP = 6 + 1 + EB, 1 + 1 + EB + 1
            ep = Chain(dve, fin_steps, 0)
            A = acc[:, 0:NT * RS].rearrange("p (k w) -> p k w", w=RS)
            cnt = A[:, :, ONE:ONE + 1]
            node_v = node_f.rearrange("p (k c) -> p k c", c=3)
            ep.done(nc.vector.tensor_scalar(deg_f[:, :, 0:1], cnt, 1.0, None, ALU.max))
            ep.done(nc.vector.tensor_scalar(deg_f[:, :, 1:2], cnt, 1.0, None, ALU.add))
            ep.done(nc.vector.tensor_scalar(node_v[:, :, 2:3], cnt, 1.0, None, ALU.min))
            ep.after()
            ep.done(nc.vector.reciprocal(node_v[:, :, 0:2], deg_f))
            ep.after()

            def scalars(b, h):
                nc.vector.tensor_scalar(sc_f[:, h, :, :].rearrange("p k c -> p (k c)"),
                                        node_f[:, bass.ds(b * (EB * 3), EB * 3)], 1.0, None, ALU.mult).then_inc(scalars_ready, 1)

            def mean_edges(b, h):
                dve.wait_ge(scalars_ready, b + 1)
                nc.vector.tensor_tensor(es_f[:, h, :, :], acc[:, bass.ds(b * (EB * RS), EB * RS)]
                                        .rearrange("p (k w) -> p k w", w=RS)[:, :, 0:D],
                                        sc_f[:, h, :, 0:1].to_broadcast([P, EB, D]), ALU.mult).then_inc(means_ready, 1)

            def attended(ep, b, h, loaded, used):
                if used is not None:
                    dve.wait_ge(out_ready, used)
                src_sums = acc[:, bass.ds(b * (EB * RS), EB * RS)].rearrange("p (k w) -> p k w", w=RS)[:, :, HF:EX]
                ep.done(nc.vector.tensor_tensor(
                    o_f[:, h, :, :].rearrange("p k (h d) -> p k h d", d=DH), src_sums.rearrange("p k (h d) -> p k h d", d=DH),
                    rden_f[:, bass.ds(b * (EB * H), EB * H)].rearrange("p (k h) -> p k h", h=H).unsqueeze(3)
                    .to_broadcast([P, EB, H, DH]), ALU.mult))
                ep.after()
                dve.wait_ge(fin_loaded[h], loaded)
                dve.wait_ge(scalars_ready, b + 1)
                for k in range(EB):
                    ep.done(nc.vector.scalar_tensor_tensor(out=o_f[:, h, k, :], in0=hf_f[:, h, k, :],
                                                           scalar=sc_f[:, h, k, 1:2], in1=o_f[:, h, k, :],
                                                           op0=ALU.mult, op1=ALU.add))

            def batch(b, h, loaded, used, more, ahead):
                ep = Chain(dve, fin_steps, b * EP + FIRST)
                st = stat_f[:, h, :, :]
                dve.wait_ge(edge_part_done, b + 1)
                ep.after()
                for a, tiles in ((0, 4), (1, EB - 4)):
                    v = o_f[:, h, 4 * a:4 * a + tiles, :]
                    nc.vector.tensor_tensor(v, v, ps_proj[h][a][:, 0:tiles * P].rearrange("p (k d) -> p k d", d=D),
                                            ALU.add).then_inc(edge_part_added, 1)
                dve.wait_ge(edge_part_added, b * 2 + 2)
                ep.done(nc.vector.tensor_reduce(st[:, SUM, :], o_f[:, h, :, :], AX.X, ALU.add))
                ep.after()
                nc.vector.tensor_scalar(st[:, NMEAN, :], st[:, SUM, :], -1.0 / D, None, ALU.mult).then_inc(mean_ready, 1)
                if more:
                    attended(ep, b + 1, 1 - h, loaded, used)
                if ahead:
                    scalars(b + 2, h)
                dve.wait_ge(squares_summed, b + 1)
                nc.vector.tensor_scalar(st[:, VAR, :], st[:, SSQ, :], 1.0 / D, LN_EPS, ALU.mult, ALU.add).then_inc(variance_ready, 1)
                dve.wait_ge(root_ready, b + 1)
                ep.done(nc.vector.reciprocal(st[:, RSTD, :], st[:, STD, :]))
                ep.after()
                nc.vector.tensor_tensor(st[:, NMR, :], st[:, NMEAN, :], st[:, RSTD, :], ALU.mult).then_inc(norm_scalars_ready, 1)
                assert ep.n == (EP if more else 2), ep.n

            for b in range(2):
                scalars(b, b)
                mean_edges(b, b)
            ep.done(nc.vector.tensor_scalar(den_f, A[:, :, EX:ROW], DEN_FLOOR, None, ALU.max))
            ep.after()
            ep.done(nc.vector.reciprocal(rden_f, den_f.rearrange("p k h -> p (k h)")))
            ep.after()
            attended(ep, 0, 0, 32, None)
            assert ep.n == FIRST, ep.n
            batch(0, 0, 32, None, True, True)
            with dve.Fori(0, (NEB - 3) // 2) as i:
                for h in range(2):
                    batch(i * 2 + (1 + h), 1 - h, i * 32 + 64, i * 2 + (1 + h), True, True)
            batch(NEB - 2, 1, NEB // 2 * 32 + 64, NEB - 2, True, False)
            batch(NEB - 1, 0, None, None, False, False)


def kernel(x, src, dst, edge_attr_128, L0_gnn_W_fc, L0_gnn_attn_l, L0_gnn_attn_r, L0_gnn_bias, L0_gnn_W_e, L0_gnn_b_e):
    import concourse.bacc as bacc
    from concourse.bass_utils import run_bass_kernel_spmd

    n, e = x.shape[0], src.shape[0]
    pad = -e % P
    past = -(-n // P) * P - 1
    arrays = {
        "x": x,
        "src": np.pad(np.asarray(src), (0, pad)),
        "dst": np.pad(np.asarray(dst), (0, pad), constant_values=past),
        "edge_attr": np.pad(np.asarray(edge_attr_128), ((0, pad), (0, 0))),
        "w_fc": L0_gnn_W_fc, "attn_l": L0_gnn_attn_l, "attn_r": L0_gnn_attn_r, "bias": L0_gnn_bias,
        "w_e": L0_gnn_W_e, "b_e": L0_gnn_b_e,
    }
    arrays = {k: np.ascontiguousarray(v) for k, v in arrays.items()}
    nc = bacc.Bacc("TRN2", target_bir_lowering=False, num_devices=1)
    args = [nc.dram_tensor(k, v.shape, mybir.dt.from_np(v.dtype), kind="ExternalInput").ap() for k, v in arrays.items()]
    out = nc.dram_tensor("out", x.shape, F32, kind="ExternalOutput").ap()
    gat_layer(nc, *args, out)
    return run_bass_kernel_spmd(nc, [arrays], core_ids=[0]).results[0]["out"]
```
